# Optimizing a Trainium2 kernel written in Bass

```python
import numpy as np
import jax
import jax.numpy as jnp

def _softmax(x, axis=-1):
    return jax.nn.softmax(x, axis=axis)

def _gelu(x):
    return jax.nn.gelu(x, approximate=True)

def _silu(x):
    return jax.nn.silu(x)

def _sigmoid(x):
    return jax.nn.sigmoid(x)

def _layernorm(x, axis=-1, eps=1e-05):
    m = jnp.mean(x, axis=axis, keepdims=True)
    v = jnp.var(x, axis=axis, keepdims=True)
    return (x - m) / jnp.sqrt(v + eps)

def _scatter_add(tgt, idx, src, axis=0):
    return tgt.at[idx].add(src)

def _segment_sum(src, seg, n):
    return jax.ops.segment_sum(src, seg, n)
kernel_name = 'mk_seq_preln_d2_jaxref_r8_03c967'

def setup_inputs(seed: int=0):
    np.random.seed(seed)
    _w = jnp.asarray

    def _L0_attn_setup():
        import jax, jax.numpy as jnp
        import numpy as np
        B, S, D = (4, 256, 256)
        N = D
        key = jax.random.key(seed)
        ks = jax.random.split(key, 6)
        x = jax.random.normal(ks[0], (B, S, D), dtype=jnp.float32)
        W_dt = jax.random.normal(ks[1], (N, D), dtype=jnp.float32) / np.sqrt(D)
        b_dt = jnp.ones((N,), dtype=jnp.float32)
        W_B = jax.random.normal(ks[2], (N, D), dtype=jnp.float32) / np.sqrt(D)
        W_C = jax.random.normal(ks[3], (D, N), dtype=jnp.float32) / np.sqrt(N)
        A_log = jax.random.normal(ks[4], (N,), dtype=jnp.float32) * 0.5 - 1.0
        D_skip = jnp.zeros((D,), dtype=jnp.float32)
        return {'x': x, 'W_dt': W_dt, 'b_dt': b_dt, 'W_B': W_B, 'W_C': W_C, 'A_log': A_log, 'D_skip': D_skip}
    _L0_attn_in = _L0_attn_setup()

    def _L0_ffn_setup():
        import jax, jax.numpy as jnp
        import numpy as np
        TOP_K = 8
        CAPACITY = 128
        key = jax.random.key(seed)
        k1, k2, k3, k4 = jax.random.split(key, 4)
        B, S, H, E, I = (2, 128, 256, 64, 96)
        hidden_states = jax.random.normal(k1, (B, S, H), dtype=jnp.float32)
        router_weight = jax.random.normal(k2, (E, H), dtype=jnp.float32) * 0.02
        gate_up_proj = jax.random.normal(k3, (E, H, 2 * I), dtype=jnp.float32) * 0.02
        down_proj = jax.random.normal(k4, (E, I, H), dtype=jnp.float32) * 0.02
        return {'hidden_states': hidden_states, 'router_weight': router_weight, 'gate_up_proj': gate_up_proj, 'down_proj': down_proj}
    _L0_ffn_in = _L0_ffn_setup()

    def _L1_attn_setup():
        import jax, jax.numpy as jnp
        import numpy as np
        H, HD, NKV = (16, 128, 4)
        SEL_TOPK, SEL_DIM, SEL_HEADS = (64, 64, 1)
        ROPE_BASE = 10000.0

        def _rope_emb(t, hd):
            inv = 1.0 / ROPE_BASE ** (jnp.arange(0, hd, 2, dtype=jnp.float32) / hd)
            freqs = jnp.arange(t, dtype=jnp.float32)[:, None] * inv[None, :]
            return jnp.concatenate([freqs, freqs], axis=-1)

        def _apply_rotary(x, rope):
            cos = jnp.cos(rope)[None, :, None, :]
            sin = jnp.sin(rope)[None, :, None, :]
            x1, x2 = (x[..., ::2], x[..., 1::2])
            c, s = (cos[..., ::2], sin[..., ::2])
            rot = jnp.stack([x1 * c - x2 * s, x1 * s + x2 * c], axis=-1)
            return rot.reshape(x.shape)

        def _selector_mask(q, k):
            b, h, t, d = q.shape
            qs = q[:, :SEL_HEADS, :, :SEL_DIM]
            ks = k[:, :SEL_HEADS, :, :SEL_DIM]
            scores = jnp.einsum('bhqd,bhkd->bhqk', qs, ks) / np.sqrt(SEL_DIM).astype(np.float32)
            future = jnp.triu(jnp.ones((t, t), bool), 1)
            scores = jnp.where(future[None, None], -jnp.inf, scores)
            idx = jax.lax.top_k(scores, SEL_TOPK)[1]
            rows = jnp.arange(t)
            scatter_row = lambda im: jnp.zeros((t, t), bool).at[rows[:, None], im].set(True)
            sel = jax.vmap(jax.vmap(scatter_row))(idx)
            sel = sel.at[:, :, rows, rows].set(True)
            sel = sel & jnp.tril(jnp.ones((t, t), bool))[None, None]
            sel = jnp.any(sel, axis=1, keepdims=True)
            return jnp.where(sel, 0.0, -jnp.inf).astype(jnp.float32)
        key = jax.random.key(seed)
        ks = jax.random.split(key, 6)
        B, T, D, LAT = (2, 256, 256, 64)
        s = 0.02
        return {'x': jax.random.normal(ks[0], (B, T, D), jnp.float32), 'Wq': jax.random.normal(ks[1], (D, H * HD), jnp.float32) * s, 'bq': jnp.zeros((H * HD,), jnp.float32), 'Wkd': jax.random.normal(ks[2], (D, LAT), jnp.float32) * s, 'bkd': jnp.zeros((LAT,), jnp.float32), 'Wku': jax.random.normal(ks[3], (LAT, 2 * NKV * HD), jnp.float32) * s, 'bku': jnp.zeros((2 * NKV * HD,), jnp.float32), 'Wo': jax.random.normal(ks[4], (H * HD, D), jnp.float32) * s, 'bo': jnp.zeros((D,), jnp.float32)}
    _L1_attn_in = _L1_attn_setup()

    def _L1_ffn_setup():
        import jax, jax.numpy as jnp
        import numpy as np
        BLOCK_SIZE = 32
        HIDDEN_SIZE = 256
        MLP_DIM = 2048
        NVFP4_LUT = jnp.array([0.0, 0.5, 1.0, 1.5, 2.0, 3.0, 4.0, 6.0, 0.0, -0.5, -1.0, -1.5, -2.0, -3.0, -4.0, -6.0], dtype=jnp.float32)

        def dequant_nvfp4(W_packed, scales, block=BLOCK_SIZE):
            N = W_packed.shape[0]
            low = W_packed & 15
            high = W_packed >> 4 & 15
            idx = jnp.stack([low, high], axis=-1).reshape(N, -1)
            vals = NVFP4_LUT[idx]
            K = vals.shape[1]
            vals = vals.reshape(N, K // block, block) * scales[:, :, None]
            return vals.reshape(N, K)
        key = jax.random.key(seed)
        ks = jax.random.split(key, 7)
        x = jax.random.normal(ks[0], (4, 32, HIDDEN_SIZE), dtype=jnp.float32)
        gate_W_packed = jax.random.randint(ks[1], (MLP_DIM, HIDDEN_SIZE // 2), 0, 32, dtype=jnp.int32)
        gate_scales = jax.random.uniform(ks[2], (MLP_DIM, HIDDEN_SIZE // BLOCK_SIZE), dtype=jnp.float32) * 0.1 + 0.001
        up_W_packed = jax.random.randint(ks[3], (MLP_DIM, HIDDEN_SIZE // 2), 0, 32, dtype=jnp.int32)
        up_scales = jax.random.uniform(ks[4], (MLP_DIM, HIDDEN_SIZE // BLOCK_SIZE), dtype=jnp.float32) * 0.1 + 0.001
        down_W_packed = jax.random.randint(ks[5], (HIDDEN_SIZE, MLP_DIM // 2), 0, 32, dtype=jnp.int32)
        down_scales = jax.random.uniform(ks[6], (HIDDEN_SIZE, MLP_DIM // BLOCK_SIZE), dtype=jnp.float32) * 0.1 + 0.001
        return {'x': x, 'gate_W_packed': gate_W_packed, 'gate_scales': gate_scales, 'up_W_packed': up_W_packed, 'up_scales': up_scales, 'down_W_packed': down_W_packed, 'down_scales': down_scales}
    _L1_ffn_in = _L1_ffn_setup()
    _d = {'L0_attn_x': _L0_attn_in['x'], 'L0_attn_W_dt': _L0_attn_in['W_dt'], 'L0_attn_b_dt': _L0_attn_in['b_dt'], 'L0_attn_W_B': _L0_attn_in['W_B'], 'L0_attn_W_C': _L0_attn_in['W_C'], 'L0_attn_A_log': _L0_attn_in['A_log'], 'L0_attn_D_skip': _L0_attn_in['D_skip'], 'L0_ffn_router_weight': _L0_ffn_in['router_weight'], 'L0_ffn_gate_up_proj': _L0_ffn_in['gate_up_proj'], 'L0_ffn_down_proj': _L0_ffn_in['down_proj'], 'L1_attn_Wq': _L1_attn_in['Wq'], 'L1_attn_bq': _L1_attn_in['bq'], 'L1_attn_Wkd': _L1_attn_in['Wkd'], 'L1_attn_bkd': _L1_attn_in['bkd'], 'L1_attn_Wku': _L1_attn_in['Wku'], 'L1_attn_bku': _L1_attn_in['bku'], 'L1_attn_Wo': _L1_attn_in['Wo'], 'L1_attn_bo': _L1_attn_in['bo'], 'L1_ffn_gate_W_packed': _L1_ffn_in['gate_W_packed'], 'L1_ffn_gate_scales': _L1_ffn_in['gate_scales'], 'L1_ffn_up_W_packed': _L1_ffn_in['up_W_packed'], 'L1_ffn_up_scales': _L1_ffn_in['up_scales'], 'L1_ffn_down_W_packed': _L1_ffn_in['down_W_packed'], 'L1_ffn_down_scales': _L1_ffn_in['down_scales']}
    _x0 = _d['L0_attn_x']
    _d['L0_attn_x'] = jax.random.normal(jax.random.fold_in(jax.random.key(seed), 1), (8, 512, 256), dtype=_x0.dtype)
    del _x0
    return _d

def reference(L0_attn_x, L0_attn_W_dt, L0_attn_b_dt, L0_attn_W_B, L0_attn_W_C, L0_attn_A_log, L0_attn_D_skip, L0_ffn_router_weight, L0_ffn_gate_up_proj, L0_ffn_down_proj, L1_attn_Wq, L1_attn_bq, L1_attn_Wkd, L1_attn_bkd, L1_attn_Wku, L1_attn_bku, L1_attn_Wo, L1_attn_bo, L1_ffn_gate_W_packed, L1_ffn_gate_scales, L1_ffn_up_W_packed, L1_ffn_up_scales, L1_ffn_down_W_packed, L1_ffn_down_scales):

    def _L0_attn_ref(x, W_dt, b_dt, W_B, W_C, A_log, D_skip):
        import jax, jax.numpy as jnp
        import numpy as np
        B, S, D = (4, 256, 256)
        N = D
        dt = jax.nn.softplus(jnp.einsum('bsd,nd->bsn', x, W_dt) + b_dt)
        Bp = jnp.einsum('bsd,nd->bsn', x, W_B)
        A = -jnp.exp(A_log)
        A_bar = jnp.exp(dt * A)
        inputs = dt * Bp * x
        h0 = jnp.zeros((x.shape[0], A_log.shape[0]), dtype=x.dtype)

        def step(h, ab_u):
            ab, u = ab_u
            h = ab * h + u
            return (h, h)
        _, h_all = jax.lax.scan(step, h0, (jnp.swapaxes(A_bar, 0, 1), jnp.swapaxes(inputs, 0, 1)))
        h_all = jnp.swapaxes(h_all, 0, 1)
        out = jnp.einsum('bsn,dn->bsd', h_all, W_C) + D_skip * x
        return out

    def _L0_ffn_ref(hidden_states, router_weight, gate_up_proj, down_proj):
        import jax, jax.numpy as jnp
        import numpy as np
        TOP_K = 8
        CAPACITY = 128
        B, S, H = hidden_states.shape
        E = router_weight.shape[0]
        K, C = (TOP_K, CAPACITY)
        x = hidden_states.reshape(-1, H)
        logits = x @ router_weight.T
        probs = jax.nn.softmax(logits, axis=-1)
        topw, topi = jax.lax.top_k(probs, K)
        topw = topw / jnp.sum(topw, axis=-1, keepdims=True)
        flat_e = topi.reshape(-1)
        oh = jax.nn.one_hot(flat_e, E, dtype=jnp.int32)
        pos = jnp.take_along_axis(jnp.cumsum(oh, axis=0), flat_e[:, None], axis=1)[:, 0] - 1
        x_rep = jnp.repeat(x, K, axis=0)
        xe = jnp.zeros((E, C, H), x.dtype).at[flat_e, pos].set(x_rep, mode='drop')
        gu = jnp.einsum('ech,ehf->ecf', xe, gate_up_proj)
        g, u = jnp.split(gu, 2, axis=-1)
        h = jax.nn.silu(g) * u
        ye = jnp.einsum('eci,eih->ech', h, down_proj)
        valid = pos < C
        y_flat = jnp.where(valid[:, None], ye[flat_e, jnp.minimum(pos, C - 1)], 0.0)
        y = jnp.sum(y_flat.reshape(-1, K, H) * topw.reshape(-1, K)[..., None], axis=1)
        return y.reshape(B, S, H)

    def _L1_attn_ref(x, Wq, bq, Wkd, bkd, Wku, bku, Wo, bo):
        import jax, jax.numpy as jnp
        import numpy as np
        H, HD, NKV = (16, 128, 4)
        SEL_TOPK, SEL_DIM, SEL_HEADS = (64, 64, 1)
        ROPE_BASE = 10000.0

        def _rope_emb(t, hd):
            inv = 1.0 / ROPE_BASE ** (jnp.arange(0, hd, 2, dtype=jnp.float32) / hd)
            freqs = jnp.arange(t, dtype=jnp.float32)[:, None] * inv[None, :]
            return jnp.concatenate([freqs, freqs], axis=-1)

        def _apply_rotary(x, rope):
            cos = jnp.cos(rope)[None, :, None, :]
            sin = jnp.sin(rope)[None, :, None, :]
            x1, x2 = (x[..., ::2], x[..., 1::2])
            c, s = (cos[..., ::2], sin[..., ::2])
            rot = jnp.stack([x1 * c - x2 * s, x1 * s + x2 * c], axis=-1)
            return rot.reshape(x.shape)

        def _selector_mask(q, k):
            b, h, t, d = q.shape
            qs = q[:, :SEL_HEADS, :, :SEL_DIM]
            ks = k[:, :SEL_HEADS, :, :SEL_DIM]
            scores = jnp.einsum('bhqd,bhkd->bhqk', qs, ks) / np.sqrt(SEL_DIM).astype(np.float32)
            future = jnp.triu(jnp.ones((t, t), bool), 1)
            scores = jnp.where(future[None, None], -jnp.inf, scores)
            idx = jax.lax.top_k(scores, SEL_TOPK)[1]
            rows = jnp.arange(t)
            scatter_row = lambda im: jnp.zeros((t, t), bool).at[rows[:, None], im].set(True)
            sel = jax.vmap(jax.vmap(scatter_row))(idx)
            sel = sel.at[:, :, rows, rows].set(True)
            sel = sel & jnp.tril(jnp.ones((t, t), bool))[None, None]
            sel = jnp.any(sel, axis=1, keepdims=True)
            return jnp.where(sel, 0.0, -jnp.inf).astype(jnp.float32)
        b, t, d = x.shape
        G = H // NKV
        q = (x @ Wq + bq).reshape(b, t, H, HD)
        kv = (x @ Wkd + bkd) @ Wku + bku
        k = kv[..., :NKV * HD].reshape(b, t, NKV, HD)
        v = kv[..., NKV * HD:].reshape(b, t, NKV, HD)
        rope = _rope_emb(t, HD)
        qb = _apply_rotary(q, rope).transpose(0, 2, 1, 3)
        kb = jnp.repeat(_apply_rotary(k, rope).transpose(0, 2, 1, 3), G, 1)
        vb = jnp.repeat(v.transpose(0, 2, 1, 3), G, 1)
        qu = jax.lax.stop_gradient(q.transpose(0, 2, 1, 3))
        ku = jnp.repeat(jax.lax.stop_gradient(k.transpose(0, 2, 1, 3)), G, 1)
        mask = _selector_mask(qu, ku)
        scores = jnp.einsum('bhqd,bhkd->bhqk', qb, kb) / np.sqrt(HD).astype(np.float32)
        attn = jax.nn.softmax(scores + mask, axis=-1)
        y = jnp.einsum('bhqk,bhkd->bhqd', attn, vb)
        y = y.transpose(0, 2, 1, 3).reshape(b, t, H * HD)
        return y @ Wo + bo

    def _L1_ffn_ref(x, gate_W_packed, gate_scales, up_W_packed, up_scales, down_W_packed, down_scales):
        import jax, jax.numpy as jnp
        import numpy as np
        BLOCK_SIZE = 32
        HIDDEN_SIZE = 256
        MLP_DIM = 2048
        NVFP4_LUT = jnp.array([0.0, 0.5, 1.0, 1.5, 2.0, 3.0, 4.0, 6.0, 0.0, -0.5, -1.0, -1.5, -2.0, -3.0, -4.0, -6.0], dtype=jnp.float32)

        def dequant_nvfp4(W_packed, scales, block=BLOCK_SIZE):
            N = W_packed.shape[0]
            low = W_packed & 15
            high = W_packed >> 4 & 15
            idx = jnp.stack([low, high], axis=-1).reshape(N, -1)
            vals = NVFP4_LUT[idx]
            K = vals.shape[1]
            vals = vals.reshape(N, K // block, block) * scales[:, :, None]
            return vals.reshape(N, K)
        B, S, H = x.shape
        xt = x.reshape(B * S, H)
        Wg = dequant_nvfp4(gate_W_packed, gate_scales)
        Wu = dequant_nvfp4(up_W_packed, up_scales)
        Wd = dequant_nvfp4(down_W_packed, down_scales)
        gate = jnp.einsum('th,nh->tn', xt, Wg)
        up = jnp.einsum('th,nh->tn', xt, Wu)
        gelu = jnp.tanh(0.7978845608028654 * (gate + 0.044715 * gate ** 3)) * gate * 0.5 + gate * 0.5
        inter = gelu * up
        out = jnp.einsum('tn,hn->th', inter, Wd)
        return out.reshape(B, S, H)
    x = L0_attn_x
    x = x + _L0_attn_ref(_layernorm(x, axis=-1), L0_attn_W_dt, L0_attn_b_dt, L0_attn_W_B, L0_attn_W_C, L0_attn_A_log, L0_attn_D_skip)
    x = x + _L0_ffn_ref(_layernorm(x, axis=-1), L0_ffn_router_weight, L0_ffn_gate_up_proj, L0_ffn_down_proj)
    x = x + _L1_attn_ref(_layernorm(x, axis=-1), L1_attn_Wq, L1_attn_bq, L1_attn_Wkd, L1_attn_bkd, L1_attn_Wku, L1_attn_bku, L1_attn_Wo, L1_attn_bo)
    x = x + _L1_ffn_ref(_layernorm(x, axis=-1), L1_ffn_gate_W_packed, L1_ffn_gate_scales, L1_ffn_up_W_packed, L1_ffn_up_scales, L1_ffn_down_W_packed, L1_ffn_down_scales)
    return x

_drawn_inputs = setup_inputs


def setup_inputs(seed=0):
    import zlib

    import numpy as np

    out = dict(_drawn_inputs(seed))
    spreads = {'L0_attn_b_dt': (1.0, 0.2),
     'L0_attn_D_skip': (0.0, 0.1),
     'L1_attn_bq': (0.0, 0.8),
     'L1_attn_bkd': (0.0, 0.8),
     'L1_attn_bku': (0.0, 0.1),
     'L1_attn_bo': (0.0, 0.1)}
    factors = {'L0_ffn_router_weight': 8.0,
     'L0_ffn_gate_up_proj': 8.0,
     'L0_ffn_down_proj': 8.0,
     'L1_attn_Wq': 8.0,
     'L1_attn_Wkd': 7.554,
     'L1_attn_Wku': 4.261}
    for name, (base, spread) in spreads.items():
        noise = np.random.default_rng([zlib.crc32(name.encode()), seed]).standard_normal(out[name].shape)
        drawn = base * np.exp(spread * noise) if base else spread * noise
        out[name] = jnp.asarray(drawn.astype(out[name].dtype))
    for name, factor in factors.items():
        out[name] = (out[name] * factor).astype(out[name].dtype)
    return out
```

```python
from contextlib import ExitStack

import numpy as np

import concourse.bass as bass
from concourse import mybir

F32 = mybir.dt.float32
BF16 = mybir.dt.bfloat16
F16 = mybir.dt.float16
I32 = mybir.dt.int32
ALU = mybir.AluOpType
ACT = mybir.ActivationFunctionType
AX = mybir.AxisListType
ds = bass.ds

P = 128
NB, S, D = 8, 512, 256
T = NB * S
TT = S // P
DC = D // P
EPS = 1e-5

NE, TOPK, CAP, FF = 64, 8, 128, 96
HI, LO = 16, 8
EG = NE // LO
ROW = D + NE
NCH = 2

NH, HD, NKV, LAT, SELD, SELK = 16, 128, 4, 64, 64, 64
G = NH // NKV
NEG = -1.0e30
GONE = -3.0e38
FN = 2048
FNC = FN // P


class Space:

    def __init__(self, nc, stack, stage=""):
        self.nc, self.stack, self.stage = nc, stack, stage
        self.sems = []

    def sb(self, name, shape, dt=F32):
        return self.stack.enter_context(self.nc.sbuf_tensor(name, shape, dt))

    def banks(self, name, n=1):
        return [self.stack.enter_context(self.nc.psum_tensor(f"{name}{i}", [P, 512], F32)) for i in range(n)]

    def sem(self, name):
        self.sems.append(self.nc.alloc_semaphore(name=self.stage + name))
        return self.sems[-1]

    def clear(self):
        self.nc.clear_and_free_semaphores(self.sems)
        self.nc.all_engine_barrier()


def stage1(nc, a, acc, xg, slots):
    xa = acc[0]
    with ExitStack() as st:
        sp = Space(nc, st, "s1_")
        sb, sem = sp.sb, sp.sem
        ident = sb("ident", [P, P])
        w_dt = sb("w_dt", [P, DC, D])
        w_b = sb("w_b", [P, DC, D])
        w_c = sb("w_c", [P, DC, D])
        w_r = sb("w_r", [P, DC, NE])
        b_dt = sb("b_dt", [P, DC])
        a_log = sb("a_log", [P, DC])
        a_exp = sb("a_exp", [P, DC])
        a_neg = sb("a_neg", [P, DC])
        dskip = sb("dskip", [P, D])
        half_neg = sb("half_neg", [P, TT])
        upto = sb("upto", [P, P], BF16)
        ones = sb("ones", [P, P], BF16)
        iota_hi = sb("iota_hi", [P, HI, NE], BF16)
        iota_lo = sb("iota_lo", [P, LO, NE], BF16)
        blank = sb("blank", [P, D])
        row1 = sb("row1", [P, 1])
        tile_no = sb("tile_no", [P, T // P])
        same_e = sb("same_e", [P, LO])
        same_hi = sb("same_hi", [P, HI])
        spread = sb("spread", [P, LO, HI, LO])
        xb = sb("xb", [P, 2, TT, D])
        xn = sb("xn", [P, 2, TT, D])
        xd = sb("xd", [P, 2, TT, D])
        stat = sb("stat", [P, TT, 6])
        mv = sb("mv", [P, TT, 2])
        veps = sb("veps", [P, TT])
        rstd = sb("rstd", [P, TT])
        xnt = sb("xnt", [P, DC, S])
        z = sb("z", [P, DC, S])
        az = sb("az", [P, DC, S])
        ez = sb("ez", [P, DC, S])
        lz = sb("lz", [P, DC, S])
        dt = sb("dt", [P, DC, S])
        abar = sb("abar", [P, DC, S])
        ub = sb("ub", [P, DC, S])
        ux = sb("ux", [P, DC, S])
        h = sb("h", [P, 2, DC, S])
        x1 = sb("x1", [P, TT, D])
        rows = sb("rows", [P, TT, ROW])
        stat2 = sb("stat2", [P, TT, 6])
        mv2 = sb("mv2", [P, TT, 2])
        veps2 = sb("veps2", [P, TT])
        rstd2 = sb("rstd2", [P, TT])
        xn2t = sb("xn2t", [P, DC, S])
        lg = sb("lg", [P, TT, NE])
        top8 = sb("top8", [P, TT, TOPK])
        lrest = sb("lrest", [P, TT, NE])
        sel = sb("sel", [P, TT, NE], BF16)
        ls = sb("ls", [P, TT, NE])
        el = sb("el", [P, TT, NE])
        es = sb("es", [P, TT, NE])
        esum = sb("esum", [P, TT])
        erec = sb("erec", [P, TT])
        bsum = sb("bsum", [P, NE])
        before = sb("before", [P, NE], BF16)
        before_f = sb("before_f", [P, NE])
        q0 = sb("q0", [P, TT, NE])
        qi = sb("qi", [P, TT, NE], I32)
        qh = sb("qh", [P, TT, NE], I32)
        ql = sb("ql", [P, TT, NE], I32)
        qhb = sb("qhb", [P, TT, NE], BF16)
        qlb = sb("qlb", [P, TT, NE], BF16)
        oh_hi = sb("oh_hi", [P, TT, HI, NE], BF16)
        oh_lo = sb("oh_lo", [P, LO, NE], BF16)
        oh_v = sb("oh_v", [P, TT, 2, LO, NE], BF16)
        slot_acc = sb("slot_acc", [P, EG, 2, LO, LO])
        slot_m = sb("slot_m", [P, EG, 2, LO, LO])
        tokf = sb("tokf", [P, 2, NE])
        tid = sb("tid", [P, NE])
        emp = sb("emp", [P, NE])
        gf = sb("gf", [P, NE])
        sf = sb("sf", [P, NE])

        bank_t = sp.banks("bank_t", 2)
        bank_d = sp.banks("bank_d", 2)
        bank_b = sp.banks("bank_b", 2)
        bank_o = sp.banks("bank_o", 2)

        consts_in = sem("consts_in")
        consts_pool = sem("consts_pool")
        x_in = [sem(f"x_in{u}") for u in range(2)]
        x_free = sem("x_free")
        rows_out = sem("rows_out")
        aexp_done = sem("aexp_done")
        aneg_done = sem("aneg_done")
        zeroed = sem("zeroed")
        stat_done = sem("stat_done")
        mv_done = sem("mv_done")
        veps_done = sem("veps_done")
        rstd_done = sem("rstd_done")
        xn_done = sem("xn_done")
        dx_done = sem("dx_done")
        xd_done = sem("xd_done")
        t_done = sem("t_done")
        xnt_done = sem("xnt_done")
        d_done = sem("d_done")
        b_done = sem("b_done")
        z_done = sem("z_done")
        az_done = sem("az_done")
        ez_done = sem("ez_done")
        lz_done = sem("lz_done")
        dt_done = sem("dt_done")
        abar_done = sem("abar_done")
        ub_done = sem("ub_done")
        ux_done = sem("ux_done")
        h_done = sem("h_done")
        o_done = sem("o_done")
        x1_done = sem("x1_done")
        stat2_done = sem("stat2_done")
        mv2_done = sem("mv2_done")
        veps2_done = sem("veps2_done")
        rstd2_done = sem("rstd2_done")
        xn2_done = sem("xn2_done")
        t2_done = sem("t2_done")
        xn2t_done = sem("xn2t_done")
        r_done = sem("r_done")
        lg_done = sem("lg_done")
        top_done = sem("top_done")
        lrest_done = sem("lrest_done")
        sel_done = sem("sel_done")
        ls_done = sem("ls_done")
        el_done = sem("el_done")
        es_done = sem("es_done")
        esum_done = sem("esum_done")
        erec_done = sem("erec_done")
        wts_done = sem("wts_done")
        pos_done = sem("pos_done")
        q0_done = sem("q0_done")
        bsum_done = sem("bsum_done")
        beforef_done = sem("beforef_done")
        before_done = sem("before_done")
        qi_done = sem("qi_done")
        qhl_done = sem("qhl_done")
        qb_done = sem("qb_done")
        hi_done = sem("hi_done")
        lo_done = sem("lo_done")
        v_done = sem("v_done")
        inv_done = sem("inv_done")
        acc_done = sem("acc_done")
        fin = sem("fin")
        fin_pe = sem("fin_pe")
        xa_out = sem("xa_out")
        acc_free = sem("acc_free")
        blank_done = sem("blank_done")
        blank_out = sem("blank_out")
        q_free = sem("q_free")
        same_done = sem("same_done")

        block = nc.Block()
        block.__enter__()

        xa_v = xa.rearrange("(b t p) d -> b p t d", t=TT, p=P)
        xg_v = xg.rearrange("(b t p) d -> b p t d", t=TT, p=P)
        x_v = a["L0_attn_x"].rearrange("b (t p) d -> b p t d", p=P)

        def one(ap):
            return ap.rearrange("o p t d -> (o p) t d")

        def first(n):
            return isinstance(n, int) and n == 1

        def last(n):
            return isinstance(n, int) and n == NB

        def seq(i, u):
            return i * 2 + u

        @block.sync
        def _(sy):
            for dst, src in ((w_dt, "w_dt_t"), (w_b, "w_b_t"), (w_c, "w_c_t"), (w_r, "w_r_t")):
                sy.dma_start(dst[:], a[src].rearrange("(c p) n -> p c n", p=P)).then_inc(consts_in, 16)
            for dst, src in ((b_dt, "b_dt"), (a_log, "a_log")):
                sy.dma_start(dst[:], a[src]).then_inc(consts_in, 16)
            sy.dma_start(dskip[:], a["L0_attn_D_skip"].partition_broadcast(P)).then_inc(consts_in, 16)
            sy.wait_ge(blank_done, 1)
            for other in acc[1:]:
                sy.dma_start(other.rearrange("(b p) d -> p b d", p=P),
                             blank[:].unsqueeze(1).broadcast_to([P, T // P, D])).then_inc(blank_out, 16)
            with sy.Fori(0, NB // 2) as i:
                for u in range(2):
                    sy.wait_ge(x_free, seq(i, u) + 1)
                    sy.dma_start(xb[:, u], one(x_v[ds(seq(i, u), 1)])).then_inc(x_in[u], 16)
            sy.wait_ge(blank_out, 16 * (NCH - 1))

        @block.gpsimd
        def _(po):
            po.sem_inc(x_free, 2)
            po.memset(blank[:], 0.0).then_inc(blank_done, 1)
            po.memset(ident[:], 0.0).then_inc(consts_pool, 1)
            po.memset(upto[:], 1.0).then_inc(consts_pool, 1)
            po.memset(ones[:], 1.0).then_inc(consts_pool, 1)
            po.memset(half_neg[:], -0.5).then_inc(consts_pool, 1)
            po.memset(same_hi[:], 1.0).then_inc(consts_pool, 1)
            po.iota(iota_hi[:], [[1, HI], [0, NE]], 0, 0, allow_small_or_imprecise_dtypes=True).then_inc(consts_pool, 1)
            po.iota(iota_lo[:], [[1, LO], [0, NE]], 0, 0, allow_small_or_imprecise_dtypes=True).then_inc(consts_pool, 1)
            po.iota(row1[:], [[0, 1]], 1, 1, allow_small_or_imprecise_dtypes=True).then_inc(consts_pool, 1)
            po.iota(tile_no[:], [[1, T // P]], 0, 0, allow_small_or_imprecise_dtypes=True).then_inc(consts_pool, 1)
            po.wait_ge(consts_pool, 9)
            po.affine_select(out=ident[:], in_=ident[:], compare_op=ALU.not_equal, fill=1.0, base=0,
                             pattern=[[-1, P]], channel_multiplier=1).then_inc(consts_pool, 1)
            po.affine_select(out=upto[:], in_=upto[:], compare_op=ALU.is_ge, fill=0.0, base=0,
                             pattern=[[1, P]], channel_multiplier=-1).then_inc(consts_pool, 1)
            po.affine_select(out=same_hi[:], in_=same_hi[:], compare_op=ALU.is_ge, fill=0.0, base=0,
                             pattern=[[-LO, HI]], channel_multiplier=1).then_inc(consts_pool, 1)
            po.wait_ge(consts_pool, 12)
            po.affine_select(out=same_hi[:], in_=same_hi[:], compare_op=ALU.is_ge, fill=0.0, base=LO - 1,
                             pattern=[[LO, HI]], channel_multiplier=-1).then_inc(consts_pool, 1)

            def front(n, u, m):
                po.wait_ge(veps_done, n)
                po.tensor_tensor(rstd[:], veps[:], half_neg[:], ALU.pow).then_inc(rstd_done, 1)
                po.wait_ge(xn_done, n)
                po.wait_ge(x_in[u], m * 16)
                po.tensor_tensor(xd[:, u], xn[:, u], dskip[:].unsqueeze(1).broadcast_to([P, TT, D]),
                                 ALU.mult).then_inc(dx_done, 1)
                po.wait_ge(dx_done, n)
                po.tensor_tensor(xd[:, u], xd[:, u], xb[:, u], ALU.add).then_inc(xd_done, 1)
                po.wait_ge(xd_done, n)
                po.sem_inc(x_free, 1)
                if not first(n):
                    po.wait_ge(h_done, (n - 1) * DC)
                for c in range(DC):
                    po.wait_ge(ub_done, (n - 1) * DC + c + 1)
                    po.tensor_tensor(ux[:, c], ub[:, c], xnt[:, c], ALU.mult).then_inc(ux_done, 1)

            def back(n, u):
                po.wait_ge(veps2_done, n)
                po.tensor_tensor(rstd2[:], veps2[:], half_neg[:], ALU.pow).then_inc(rstd2_done, 1)

            po.wait_ge(consts_in, 16 * 7)
            front(1, 0, 1)
            with po.Fori(0, NB // 2 - 1) as i:
                for u in range(2):
                    front(seq(i, u) + 2, 1 - u, i + 1 + u)
                    back(seq(i, u) + 1, u)
            front(NB, 1, NB // 2)
            back(NB - 1, 0)
            back(NB, 1)

        @block.scalar
        def _(ac):
            ac.wait_ge(consts_in, 16 * 7)
            ac.activation(a_exp[:], a_log[:], ACT.Exp).then_inc(aexp_done, 1)
            ac.wait_ge(aexp_done, 1)
            ac.mul(a_neg[:], a_exp[:], -1.0).then_inc(aneg_done, 1)
            ac.wait_ge(aneg_done, 1)

            def front(n, u, m):
                k = (n - 1) * DC
                if not first(n):
                    ac.wait_ge(ux_done, k)
                    ac.wait_ge(h_done, k)
                for c in range(DC):
                    ac.wait_ge(t_done, k + c + 1)
                    ac.copy(xnt[:, c], bank_t[c][:]).then_inc(xnt_done, 1)
                for c in range(DC):
                    ac.wait_ge(d_done, k + c + 1)
                    ac.activation(z[:, c], bank_d[c][:], ACT.Identity, bias=b_dt[:, c:c + 1]).then_inc(z_done, 1)
                for c in range(DC):
                    ac.wait_ge(z_done, k + c + 1)
                    ac.activation(az[:, c], z[:, c], ACT.Abs).then_inc(az_done, 1)
                for c in range(DC):
                    ac.wait_ge(az_done, k + c + 1)
                    ac.activation(ez[:, c], az[:, c], ACT.Exp, scale=-1.0).then_inc(ez_done, 1)
                for c in range(DC):
                    ac.wait_ge(ez_done, k + c + 1)
                    ac.activation(lz[:, c], ez[:, c], ACT.Ln, bias=1.0).then_inc(lz_done, 1)
                for c in range(DC):
                    ac.wait_ge(dt_done, k + c + 1)
                    ac.activation(abar[:, c], dt[:, c], ACT.Exp, scale=a_neg[:, c:c + 1]).then_inc(abar_done, 1)

            def back(n, u):
                for c in range(DC):
                    ac.wait_ge(t2_done, (n - 1) * DC + c + 1)
                    ac.copy(xn2t[:, c], bank_t[c][:]).then_inc(xn2t_done, 1)
                ac.wait_ge(ls_done, n)
                ac.activation(el[:], ls[:], ACT.Exp).then_inc(el_done, 1)
                ac.wait_ge(wts_done, n)
                ac.wait_ge(x1_done, n * 2)
                ac.dma_start(one(xg_v[ds(n - 1, 1)]), rows[:]).then_inc(rows_out, 16)
                ac.dma_start(one(xa_v[ds(n - 1, 1)]), x1[:]).then_inc(xa_out, 16)

            front(1, 0, 1)
            with ac.Fori(0, NB // 2 - 1) as i:
                for u in range(2):
                    front(seq(i, u) + 2, 1 - u, i + 1 + u)
                    back(seq(i, u) + 1, u)
            front(NB, 1, NB // 2)
            back(NB - 1, 0)
            back(NB, 1)
            ac.wait_ge(rows_out, 16 * (NB + 1))
            ac.wait_ge(xa_out, 16 * (NB + 1))

        @block.tensor
        def _(pe):
            pe.wait_ge(consts_in, 16 * 7)
            pe.wait_ge(consts_pool, 13)

            def front(n, u, m):
                k = (n - 1) * DC
                pe.wait_ge(xn_done, n)
                for c in range(DC):
                    for t in range(TT):
                        mm = pe.transpose(bank_t[c][:, t * P:(t + 1) * P], xn[:, u, t, c * P:(c + 1) * P], ident[:])
                    mm.then_inc(t_done, 1)
                pe.wait_ge(xnt_done, k + DC)
                if not first(n):
                    pe.wait_ge(z_done, k)
                    pe.wait_ge(ub_done, k)
                    pe.wait_ge(acc_free, n - 1)
                for w, banks, done in ((w_dt, bank_d, d_done), (w_b, bank_b, b_done)):
                    for m in range(DC):
                        for c in range(DC):
                            mm = pe.matmul(banks[m][:], w[:, c, m * P:(m + 1) * P], xnt[:, c],
                                           start=(c == 0), stop=(c == DC - 1))
                        mm.then_inc(done, 1)

            def back(n, u):
                k = (n - 1) * DC
                pe.wait_ge(h_done, k + DC)
                pe.wait_ge(q_free, n)
                for half in range(2):
                    for t in range(2):
                        tt = half * 2 + t
                        for c in range(DC):
                            mm = pe.matmul(bank_o[half][:, t * D:(t + 1) * D], h[:, u, c, tt * P:(tt + 1) * P],
                                           w_c[:, c], start=(c == 0), stop=(c == DC - 1))
                    mm.then_inc(o_done, 1)
                pe.wait_ge(xn2_done, n)
                for c in range(DC):
                    for t in range(TT):
                        mm = pe.transpose(bank_t[c][:, t * P:(t + 1) * P], rows[:, t, c * P:(c + 1) * P], ident[:])
                    mm.then_inc(t2_done, 1)
                pe.wait_ge(xn2t_done, k + DC)
                for t in range(TT):
                    for c in range(DC):
                        mm = pe.matmul(bank_o[0][:, t * NE:(t + 1) * NE], xn2t[:, c, t * P:(t + 1) * P],
                                       w_r[:, c], start=(c == 0), stop=(c == DC - 1))
                mm.then_inc(r_done, 1)
                pe.wait_ge(sel_done, n)
                pe.wait_ge(before_done, n)
                opening = True
                for t in range(TT):
                    for lhs, rhs in [(upto, sel[:, t]), (ones, before[:])] + [(ones, sel[:, s]) for s in range(t)]:
                        mm = pe.matmul(bank_o[1][:, t * NE:(t + 1) * NE], lhs[:], rhs, start=opening, stop=False,
                                       skip_group_check=True)
                        opening = False
                mm.then_inc(pos_done, 1)
                pe.wait_ge(hi_done, n * TT)
                pe.wait_ge(v_done, n * TT * 2)
                if not last(n):
                    pe.wait_ge(ub_done, k + 2 * DC)
                for half in range(2):
                    for gg in range(EG // 2):
                        g = half * (EG // 2) + gg
                        for t in range(TT):
                            mm = pe.matmul(bank_b[half][:, gg * 128:(gg + 1) * 128],
                                           oh_hi[:, t].rearrange("p h e -> p (h e)")[:, g::LO],
                                           oh_v[:, t].rearrange("p v l e -> p (v l e)")[:, g::LO],
                                           start=(gg == 0 and t == 0), stop=(t == TT - 1), skip_group_check=True)
                    mm.then_inc(inv_done, 1)

            front(1, 0, 1)
            with pe.Fori(0, NB // 2 - 1) as i:
                for u in range(2):
                    front(seq(i, u) + 2, 1 - u, i + 1 + u)
                    back(seq(i, u) + 1, u)
            front(NB, 1, NB // 2)
            back(NB - 1, 0)
            back(NB, 1)
            pe.wait_ge(fin, 2)
            for lo in range(LO):
                mm = pe.matmul(bank_t[0][:, 0:2 * NE], spread[:, lo],
                               slot_m[:, :, :, lo, :].rearrange("p g v e -> p v e g"),
                               start=(lo == 0), stop=(lo == LO - 1))
            mm.then_inc(fin_pe, 1)

        @block.vector
        def _(ve):
            ve.memset(before[:], 0.0).then_inc(zeroed, 1)
            ve.memset(before_f[:], 0.0).then_inc(zeroed, 1)
            ve.memset(slot_acc[:], 0.0).then_inc(zeroed, 1)
            ve.wait_ge(zeroed, 3)
            ve.sem_inc(before_done, 1)
            ve.sem_inc(acc_free, 1)
            ve.sem_inc(q_free, 1)
            ve.sem_inc(rows_out, 16)
            ve.sem_inc(xa_out, 16)
            ve.wait_ge(consts_pool, 13)
            ve.tensor_reduce(same_e[:], ident[:].rearrange("p (h j) -> p j h", j=LO), AX.X, ALU.add).then_inc(same_done, 1)

            def alone(ve):
                ve.nop(nofuse=True)

            def norm(src, st_, mv_, ve_, rs_, dst, n, sems):
                s_stat, s_mv, s_ve, s_rs, s_out = sems
                for t in range(TT):
                    ve.bn_stats(st_[:, t], src(t)).then_inc(s_stat, 1)
                for t in range(TT):
                    ve.wait_ge(s_stat, (n - 1) * TT + t + 1)
                    alone(ve)
                    ve.bn_aggr(mv_[:, t], st_[:, t]).then_inc(s_mv, 1)
                ve.wait_ge(s_mv, n * TT)
                ve.tensor_scalar(ve_[:], mv_[:, :, 1], EPS, None, ALU.add).then_inc(s_ve, 1)
                ve.wait_ge(s_rs, n)
                for t in range(TT):
                    ins = ve.tensor_scalar(dst(t), src(t), mv_[:, t, 0:1], rs_[:, t:t + 1], ALU.subtract, ALU.mult)
                ins.then_inc(s_out, 1)

            def front(n, u, m):
                k = (n - 1) * DC
                ve.wait_ge(x_in[u], m * 16)
                norm(lambda t: xb[:, u, t], stat, mv, veps, rstd, lambda t: xn[:, u, t], n,
                     (stat_done, mv_done, veps_done, rstd_done, xn_done))
                for c in range(DC):
                    ve.wait_ge(lz_done, k + c + 1)
                    ve.scalar_tensor_tensor(out=dt[:, c], in0=z[:, c], scalar=0.0, in1=lz[:, c],
                                            op0=ALU.max, op1=ALU.add).then_inc(dt_done, 1)
                for c in range(DC):
                    ve.wait_ge(dt_done, k + c + 1)
                    ve.wait_ge(b_done, k + c + 1)
                    ve.tensor_tensor(ub[:, c], bank_b[c][:], dt[:, c], ALU.mult).then_inc(ub_done, 1)
                for c in range(DC):
                    ve.wait_ge(ux_done, k + c + 1)
                    ve.wait_ge(abar_done, k + c + 1)
                    ve.tensor_tensor_scan(h[:, u, c], abar[:, c], ux[:, c], 0.0, ALU.mult, ALU.add).then_inc(h_done, 1)

            def back(n, u):
                k = (n - 1) * DC
                ve.wait_ge(rows_out, n * 16)
                ve.wait_ge(xa_out, n * 16)
                for half in range(2):
                    ve.wait_ge(o_done, (n - 1) * 2 + half + 1)
                    ve.wait_ge(xd_done, n)
                    t0 = half * 2
                    ve.tensor_tensor(x1[:, t0:t0 + 2].rearrange("p t d -> p (t d)"), bank_o[half][:],
                                     xd[:, u, t0:t0 + 2].rearrange("p t d -> p (t d)"), ALU.add).then_inc(x1_done, 1)
                ve.wait_ge(x1_done, n * 2)
                norm(lambda t: x1[:, t], stat2, mv2, veps2, rstd2, lambda t: rows[:, t, 0:D], n,
                     (stat2_done, mv2_done, veps2_done, rstd2_done, xn2_done))
                ve.wait_ge(r_done, n)
                ve.tensor_copy(lg[:].rearrange("p t e -> p (t e)"), bank_o[0][:, 0:TT * NE]).then_inc(lg_done, 1)
                ve.wait_ge(lg_done, n)
                alone(ve)
                for t in range(TT):
                    ve.max(top8[:, t], lg[:, t]).then_inc(top_done, 1)
                for t in range(TT):
                    ve.wait_ge(top_done, (n - 1) * TT + t + 1)
                    alone(ve)
                    ve.match_replace(lrest[:, t], top8[:, t], lg[:, t], GONE).then_inc(lrest_done, 1)
                ve.tensor_tensor(ls[:], lg[:], top8[:, :, 0:1].broadcast_to([P, TT, NE]), ALU.subtract).then_inc(ls_done, 1)
                ve.wait_ge(lrest_done, n * TT)
                ve.tensor_tensor(sel[:], lg[:], lrest[:], ALU.not_equal).then_inc(sel_done, 1)
                ve.wait_ge(sel_done, n)
                ve.wait_ge(el_done, n)
                ve.tensor_tensor(es[:], el[:], sel[:], ALU.mult).then_inc(es_done, 1)
                ve.wait_ge(es_done, n)
                ve.tensor_reduce(esum[:], es[:], AX.X, ALU.add).then_inc(esum_done, 1)
                ve.wait_ge(esum_done, n)
                ve.reciprocal(erec[:], esum[:]).then_inc(erec_done, 1)
                ve.wait_ge(erec_done, n)
                ve.tensor_tensor(rows[:, :, D:ROW], es[:], erec[:].unsqueeze(2).broadcast_to([P, TT, NE]),
                                 ALU.mult).then_inc(wts_done, 1)
                ve.wait_ge(pos_done, n)
                ve.scalar_tensor_tensor(out=q0[:].rearrange("p t e -> p (t e)"), in0=sel[:].rearrange("p t e -> p (t e)"),
                                        scalar=-1024.0, in1=bank_o[1][:, 0:TT * NE], op0=ALU.mult, op1=ALU.add)\
                    .then_inc(q0_done, 1)
                ve.tensor_reduce(bsum[:], sel[:].rearrange("p t e -> p e t"), AX.X, ALU.add).then_inc(bsum_done, 1)
                ve.wait_ge(q0_done, n)
                ve.sem_inc(q_free, 1)
                ve.tensor_scalar(qi[:], q0[:], 1023.0, None, ALU.add).then_inc(qi_done, 1)
                ve.wait_ge(bsum_done, n)
                ve.tensor_tensor(before_f[:], before_f[:], bsum[:], ALU.add).then_inc(beforef_done, 1)
                ve.wait_ge(qi_done, n)
                ve.tensor_scalar(qh[:], qi[:], 3, None, ALU.arith_shift_right).then_inc(qhl_done, 1)
                ve.tensor_scalar(ql[:], qi[:], LO - 1, None, ALU.bitwise_and).then_inc(qhl_done, 1)
                ve.wait_ge(beforef_done, n)
                ve.tensor_copy(before[:], before_f[:]).then_inc(before_done, 1)
                ve.wait_ge(qhl_done, 2 * n)
                ve.tensor_copy(qhb[:], qh[:]).then_inc(qb_done, 1)
                ve.tensor_copy(qlb[:], ql[:]).then_inc(qb_done, 1)
                ve.wait_ge(qb_done, 2 * n)
                for t in range(TT):
                    ve.tensor_tensor(oh_hi[:, t], qhb[:, t].unsqueeze(1).broadcast_to([P, HI, NE]), iota_hi[:],
                                     ALU.is_equal).then_inc(hi_done, 1)
                    m = (n - 1) * TT + t
                    ve.tensor_tensor(oh_lo[:], qlb[:, t].unsqueeze(1).broadcast_to([P, LO, NE]), iota_lo[:],
                                     ALU.is_equal).then_inc(lo_done, 1)
                    ve.wait_ge(lo_done, m + 1)
                    ve.tensor_scalar(oh_v[:, t, 0], oh_lo[:], row1[:, 0:1], None, ALU.mult).then_inc(v_done, 1)
                    ve.tensor_scalar(oh_v[:, t, 1], oh_lo[:], tile_no[:, ds(m, 1)], None, ALU.mult).then_inc(v_done, 1)
                    ve.wait_ge(v_done, 2 * m + 2)
                for half in range(2):
                    ve.wait_ge(inv_done, (n - 1) * 2 + half + 1)
                    part = slot_acc[:, half * (EG // 2):(half + 1) * (EG // 2)].rearrange("p g v l e -> p (g v l e)")
                    ve.tensor_tensor(part, bank_b[half][:], part, ALU.add).then_inc(acc_done, 1)
                ve.wait_ge(acc_done, 2 * n)
                ve.sem_inc(acc_free, 1)

            front(1, 0, 1)
            with ve.Fori(0, NB // 2 - 1) as i:
                for u in range(2):
                    front(seq(i, u) + 2, 1 - u, i + 1 + u)
                    back(seq(i, u) + 1, u)
            front(NB, 1, NB // 2)
            back(NB - 1, 0)
            back(NB, 1)
            ve.wait_ge(same_done, 1)
            ve.tensor_tensor(slot_m[:].rearrange("p g v l e -> p (g v l) e"),
                             slot_acc[:].rearrange("p g v l e -> p (g v l) e"),
                             same_e[:].unsqueeze(1).broadcast_to([P, EG * 2 * LO, LO]), ALU.mult).then_inc(fin, 1)
            ve.memset(spread[:], 0.0).then_inc(zeroed, 1)
            ve.wait_ge(zeroed, 4)
            for lo in range(LO):
                ins = ve.tensor_copy(spread[:, lo, :, lo], same_hi[:])
            ins.then_inc(fin, 1)
            ve.wait_ge(fin_pe, 1)
            ve.tensor_copy(tokf[:].rearrange("p v e -> p (v e)"), bank_t[0][:, 0:2 * NE]).then_inc(fin, 1)
            ve.wait_ge(fin, 3)
            ve.scalar_tensor_tensor(out=tid[:], in0=tokf[:, 1], scalar=float(P), in1=tokf[:, 0],
                                    op0=ALU.mult, op1=ALU.add).then_inc(fin, 1)
            ve.tensor_scalar(emp[:], tokf[:, 0], 0.5, float(2 * T), ALU.is_lt, ALU.mult).then_inc(fin, 1)
            ve.wait_ge(fin, 5)
            ve.tensor_scalar(gf[:], tid[:], -1.0, 0.0, ALU.add, ALU.max).then_inc(fin, 1)
            ve.scalar_tensor_tensor(out=sf[:], in0=tid[:], scalar=-1.0, in1=emp[:], op0=ALU.add, op1=ALU.add)\
                .then_inc(fin, 1)
            ve.wait_ge(fin, 7)
            ve.tensor_copy(slots[:, :, 0], gf[:]).then_inc(fin, 1)
            ve.tensor_copy(slots[:, :, 1], sf[:]).then_inc(fin, 1)
            ve.wait_ge(fin, 9)

        block.__exit__(None, None, None)
        sp.clear()


def stage2(nc, a, acc, xg, slots, wffn):
    R = 4
    PIECE = 3 * FN // NE
    with ExitStack() as st:
        sp = Space(nc, st, "s2_")
        sb, sem = sp.sb, sp.sem
        ident = sb("ident2", [P, P])
        w_gu = sb("w_gu", [P, R, DC, 2 * FF])
        w_dn = sb("w_dn", [P, R, D])
        gidx = sb("gidx", [P, R, 1], I32)
        sidx = sb("sidx", [P, R, 1], I32)
        xe = sb("xe", [P, R, ROW])
        xet = sb("xet", [P, 2, DC, P])
        sg = sb("sg", [P, 2, P])
        hh = sb("hh", [P, 2, P])
        ys = sb("ys", [P, R, D])
        codes = sb("codes", [P, 3 * FN], I32)
        scales = sb("scales", [P, 3 * FN])
        mag = sb("mag", [P, 2, PIECE], I32)
        sgn = sb("sgn", [P, 2, PIECE], I32)
        va = sb("va", [P, 2, PIECE])
        vb = sb("vb", [P, 2, PIECE])
        vc = sb("vc", [P, 2, PIECE])
        vd = sb("vd", [P, 2, PIECE])
        bank_t = sp.banks("bank2_t", 2)
        bank_g = sp.banks("bank2_g", 2)
        bank_y = sp.banks("bank2_y", 2)

        id0 = sem("id0")
        id_done = sem("id_done")
        w_in = [sem(f"w_in{j}") for j in range(R)]
        codes_in = sem("codes_in")
        gidx_done = sem("gidx_done")
        sidx_done = sem("sidx_done")
        va2_done = sem("va2_done")
        xe_in = [sem(f"xe_in{j}") for j in range(R)]
        t_done = sem("te_done")
        xet_done = sem("xet_done")
        gu_done = sem("gu_done")
        sg_done = sem("sg_done")
        hh_done = sem("hh_done")
        y_done = sem("y_done")
        ys_done = sem("ys_done")
        added = [sem(f"added{j}") for j in range(NCH)]
        mag_done = sem("mag_done")
        va_done = sem("va_done")
        vb_done = sem("vb_done")
        vc_done = sem("vc_done")
        vd_done = sem("vd_done")
        wffn_done = sem("wffn_done")

        gu_v = a["L0_ffn_gate_up_proj"].rearrange("e (c p) f -> e p c f", p=P)
        dn_v = a["L0_ffn_down_proj"]
        codes_d, scales_d = a["codes"], a["scales"]

        block = nc.Block()
        block.__enter__()

        def known(e):
            return isinstance(e, int)

        def adds(i, j):
            return i * (R // NCH) + j // NCH

        def past(eng, sem_, value):
            if not known(value) or value > 0:
                eng.wait_ge(sem_, value)

        def steps(eng, step):
            for j in range(R):
                step(j, j, 0)
            with eng.Fori(1, NE // R - 1) as i:
                for j in range(R):
                    step(i * R + j, j, i)
            for j in range(R):
                step(NE - R + j, j, NE // R - 1)

        @block.sync
        def _(sy):
            def load(e, j):
                sy.dma_start(w_gu[:, j], gu_v[ds(e, 1)].rearrange("o p c f -> (o p) c f")).then_inc(w_in[j], 16)
                sy.dma_start(w_dn[0:FF, j], dn_v[ds(e, 1)].rearrange("o f d -> (o f) d")).then_inc(w_in[j], 16)

            for j in range(R):
                load(j, j)
            sy.dma_start(codes[:], codes_d).then_inc(codes_in, 16)
            for b in range(P // 16):
                sy.dma_start(scales[b * 16:(b + 1) * 16], scales_d[b].partition_broadcast(16)).then_inc(codes_in, 16)
            with sy.Fori(0, NE // R - 1) as i:
                for j in range(R):
                    sy.wait_ge(y_done, i * R + j + 1)
                    load(i * R + j + R, j)

        @block.gpsimd
        def _(po):
            po.memset(ident[:], 0.0).then_inc(id0, 1)
            po.wait_ge(id0, 1)
            po.affine_select(out=ident[:], in_=ident[:], compare_op=ALU.not_equal, fill=1.0, base=0,
                             pattern=[[-1, P]], channel_multiplier=1).then_inc(id_done, 1)

            def gather(e, j):
                po.wait_ge(gidx_done, e + 1)
                po.nop(nofuse=True)
                po.indirect_dma_start(xe[:, j], None, xg, bass.IndirectOffsetOnAxis(ap=gidx[:, j], axis=0))\
                    .then_inc(xe_in[j], 16)

            def scatter(e, j, i):
                po.wait_ge(ys_done, e + 1)
                po.wait_ge(sidx_done, e + 1)
                c = j % NCH
                past(po, added[c], adds(i, j) * 16)
                po.nop(nofuse=True)
                po.indirect_dma_start(acc[c], bass.IndirectOffsetOnAxis(ap=sidx[:, j], axis=0), ys[:, j], None,
                                      bounds_check=T - 1, oob_is_err=False, compute_op=ALU.add)\
                    .then_inc(added[c], 16)

            for j in range(R - 1):
                gather(j, j)

            def step(e, j, i):
                if not known(e) or e + R - 1 < NE:
                    gather(e + R - 1, (j + R - 1) % R)
                scatter(e, j, i)

            steps(po, step)
            for c in range(NCH):
                po.wait_ge(added[c], 16 * (NE // NCH))

        @block.scalar
        def _(ac):
            def turned(e, j):
                ac.wait_ge(t_done, e + 1)
                ac.copy(xet[:, j % 2].rearrange("p c s -> p (c s)"), bank_t[j % 2][:, 0:DC * P]).then_inc(xet_done, 1)

            def gate(e, j):
                ac.wait_ge(gu_done, e + 1)
                ac.activation(sg[0:FF, j % 2], bank_g[j % 2][0:FF, 0:P], ACT.Silu).then_inc(sg_done, 1)

            def weigh(e, j):
                ac.wait_ge(y_done, e + 1)
                ac.activation(ys[:, j], bank_y[j % 2][:, 0:D], ACT.Copy, scale=xe[:, j, ds(e + D, 1)])\
                    .then_inc(ys_done, 1)

            def step(e, j, i):
                if not known(e) or e + 2 < NE:
                    turned(e + 2, j + 2)
                if not known(e) or e + 1 < NE:
                    gate(e + 1, j + 1)
                past(ac, added[j % NCH], (adds(i, j) - 1) * 16)
                weigh(e, j)

            turned(0, 0)
            turned(1, 1)
            gate(0, 0)
            steps(ac, step)

        @block.tensor
        def _(pe):
            pe.wait_ge(id_done, 1)

            def turn(e, j, i):
                pe.wait_ge(xe_in[j % R], i * 16 + 16)
                for c in range(DC):
                    mm = pe.transpose(bank_t[j % 2][:, c * P:(c + 1) * P], xe[:, j % R, c * P:(c + 1) * P], ident[:])
                mm.then_inc(t_done, 1)

            def gate_up(e, j, i):
                pe.wait_ge(xet_done, e + 1)
                pe.wait_ge(w_in[j % R], i * 32 + 32)
                for part in range(2):
                    for c in range(DC):
                        mm = pe.matmul(bank_g[j % 2][0:FF, part * P:(part + 1) * P],
                                       w_gu[:, j % R, c, part * FF:(part + 1) * FF], xet[:, j % 2, c],
                                       start=(c == 0), stop=(c == DC - 1))
                mm.then_inc(gu_done, 1)

            def down(e, j):
                pe.wait_ge(hh_done, e + 1)
                pe.matmul(bank_y[j % 2][:, 0:D], hh[0:FF, j % 2], w_dn[0:FF, j], start=True, stop=True)\
                    .then_inc(y_done, 1)

            def step(e, j, i):
                if not known(e) or e + 2 < NE:
                    turn(e + 2, j + 2, i + (j + 2) // R)
                if not known(e) or e + 1 < NE:
                    gate_up(e + 1, j + 1, i + (j + 1) // R)
                down(e, j)

            turn(0, 0, 0)
            turn(1, 1, 0)
            gate_up(0, 0, 0)
            steps(pe, step)

        @block.vector
        def _(ve):
            def gather_index(e, j):
                ve.tensor_copy(gidx[:, j], slots[:, ds(e, 1), 0]).then_inc(gidx_done, 1)

            def scatter_index(e, j):
                ve.tensor_copy(sidx[:, j], slots[:, ds(e, 1), 1]).then_inc(sidx_done, 1)

            def hidden(e, j):
                ve.wait_ge(sg_done, e + 1)
                ve.tensor_tensor(hh[0:FF, j % 2], bank_g[j % 2][0:FF, P:2 * P], sg[0:FF, j % 2], ALU.mult)\
                    .then_inc(hh_done, 1)

            def dequantise(e):
                w = codes[:, ds(e * PIECE, PIECE)]
                ve.tensor_scalar(mag[:, 0], w, 7, None, ALU.bitwise_and).then_inc(mag_done, 1)
                ve.tensor_scalar(mag[:, 1], w, 4, 7, ALU.arith_shift_right, ALU.bitwise_and).then_inc(mag_done, 1)
                ve.tensor_scalar(sgn[:, 0], w, 8, None, ALU.bitwise_and).then_inc(mag_done, 1)
                ve.tensor_scalar(sgn[:, 1], w, 4, 8, ALU.arith_shift_right, ALU.bitwise_and).then_inc(mag_done, 1)
                ve.wait_ge(mag_done, e * 4 + 4)
                ve.tensor_scalar(va[:], mag[:], 2.0, -8.0, ALU.mult, ALU.add).then_inc(va_done, 1)
                ve.tensor_scalar(vd[:], sgn[:], -0.25, 1.0, ALU.mult, ALU.add).then_inc(vd_done, 1)
                ve.wait_ge(va_done, e + 1)
                ve.scalar_tensor_tensor(out=vb[:], in0=mag[:], scalar=-2.0, in1=va[:], op0=ALU.add, op1=ALU.max)\
                    .then_inc(vb_done, 1)
                ve.wait_ge(vb_done, e + 1)
                ve.scalar_tensor_tensor(out=vc[:], in0=mag[:], scalar=0.5, in1=vb[:], op0=ALU.mult, op1=ALU.max)\
                    .then_inc(vc_done, 1)
                ve.wait_ge(vc_done, e + 1)
                ve.wait_ge(vd_done, e + 1)
                ve.tensor_tensor(va[:], vc[:], vd[:], ALU.mult).then_inc(va2_done, 1)
                ve.wait_ge(va2_done, e + 1)
                ve.tensor_tensor(wffn[:, :, ds(e * PIECE, PIECE)], va[:],
                                 scales[:, ds(e * PIECE, PIECE)].unsqueeze(1).broadcast_to([P, 2, PIECE]),
                                 ALU.mult).then_inc(wffn_done, 1)

            def step(e, j, i):
                if not known(e) or e + 1 < NE:
                    hidden(e + 1, j + 1)
                if not known(e) or e + R - 1 < NE:
                    gather_index(e + R - 1, (j + R - 1) % R)
                past(ve, added[j % NCH], (adds(i, j) - 1) * 16)
                scatter_index(e, j)
                dequantise(e)

            for j in range(R - 1):
                gather_index(j, j)
            hidden(0, 0)
            ve.wait_ge(codes_in, 16 * (1 + P // 16))
            steps(ve, step)
            ve.wait_ge(wffn_done, NE)

        block.__exit__(None, None, None)
        sp.clear()


def stage3(nc, a, acc, wffn, out):
    H2 = HD // 2
    QS = float(HD) ** -0.5
    AUG = LAT + 1
    WIDE = S + (TT - 1) * P
    with ExitStack() as st:
        sp = Space(nc, st, "s3_")
        sb, sem = sp.sb, sp.sem
        ident = sb("ident3", [P, P])
        half_neg = sb("half_neg3", [P, TT])
        zero_w = sb("zero_w", [P, P], BF16)
        zero_m = sb("zero_m", [P, S], BF16)
        wq = sb("wq", [P, DC, NH * HD])
        wqs = sb("wqs", [P, 4, DC, HD])
        wst = sb("wst", [P, 4, 2, 2, P])
        wqsel = sb("wqsel", [P, DC, SELD])
        wkd = sb("wkd", [P, DC, LAT])
        wkk = sb("wkk", [P, NKV, HD])
        wksel = sb("wksel", [P, SELD])
        bq = sb("bq", [P, NH])
        bk = sb("bk", [P, NKV])
        bkd = sb("bkd", [P, 1])
        bqsel = sb("bqsel", [P, 1])
        bksel = sb("bksel", [P, 1])
        rcos = sb("rcos", [P, S])
        rsin = sb("rsin", [P, S])
        wvo = sb("wvo", [P, NH // 2, D])
        obias = sb("obias", [P, D])
        bv_sb = sb("bv_sb", [P, NKV])
        causal = sb("causal", [P, WIDE])
        offdiag = sb("offdiag", [P, WIDE])
        bnbuf = sb("bnbuf", [P, TT, 6])
        bnbuf4 = sb("bnbuf4", [P, TT, 6])
        mv3 = sb("mv3", [P, TT, 2])
        mv4 = sb("mv4", [P, TT, 2])
        veps3 = sb("veps3", [P, TT])
        veps4 = sb("veps4", [P, TT])
        rstd3 = sb("rstd3", [P, TT])
        rstd4 = sb("rstd4", [P, TT])
        xin = [sb(f"xin{c}", [P, TT, D]) for c in range(NCH)]
        xn3 = sb("xn3", [P, TT, D])
        xo = sb("xo", [P, TT, D])
        x4 = sb("x4", [P, TT, D])
        xn4 = sb("xn4", [P, TT, D])
        xn3t = sb("xn3t", [P, DC, S])
        xn4t = sb("xn4t", [P, 2, S])
        kvdt = sb("kvdt", [P, S])
        kva = sb("kva", [P, TT, AUG])
        qsel = sb("qsel", [P, S])
        ksel = sb("ksel", [P, S])
        qst = sb("qst", [P, P])
        kr = sb("kr", [P, NKV, S])
        qa = sb("qa", [P, S])
        qb = sb("qb", [P, S])
        qr = sb("qr", [P, 4, S])
        mask = sb("mask", [P, TT, S])
        s0 = sb("s0", [P, S])
        m8 = sb("m8", [P, 8])
        sm = sb("sm", [P, 2, S])
        nm = sb("nm", [P, 2, 1])
        pr = sb("pr", [P, TT, S])
        pt = sb("pt", [P, 2, S])
        rec = sb("rec", [P, TT])
        ym = sb("ym", [P, TT, NH, LAT])
        gl, it = pr[:, 0:2], pr[:, 2:4]
        yt = qr[:].rearrange("p j n -> p (j n)").rearrange("p (s c q) -> p s c q", s=2, c=NH // 2)
        sr = sm
        eq, eo = pt[:, 0], pt[:, 1]
        ka, kb = qa, qb
        xs, ob = xin[0], xn4
        bvb = xn4[:, 0:2].rearrange("p t d -> p (t d)").rearrange("p (g q) -> p g q", g=NKV)
        bo_sb = x4[:, 0]
        wvt_sb = x4[:, 1].rearrange("p (g l) -> p g l", g=NKV)
        wo_sb = ym[:].rearrange("p t h l -> p (t h l)").rearrange("p (h d) -> p h d", h=NH)

        bq_ = sp.banks("bank3_q", 2)
        bs = sp.banks("bank3_s", 2)
        bp = sp.banks("bank3_p", 2)
        by = sp.banks("bank3_y", 2)

        names = """w3_in c0 c3 wvt_done wvo_done ob_ready obias_done xs_done xt_done stat3 agg3 ve3 rs3 xn3_done xo_done
            t3_done xn3t_done kvd_done kvdt_done kvt_done kva_done qk_done qksel_done k_done krope_a krope_done kr_done
            q_done qrope_a qrope_done qr_done s_done ttr_done exp_done tp_done pte_done pv_done rec_done norm_done
            yt_done yte_done o_done x4_done stat4 agg4 ve4 rs4 xn4_done t4_done xn4t_done
            qst_done ms_done s0_done mx_done mr_done eq_done eo_done mask_done
            g_done u_done gelu_done inter_done dn_done fo_done out_done""".split()
        sems = {n: sem(n) for n in names}
        (w3_in, c0, c3, wvt_done, wvo_done, ob_ready, obias_done, xs_done, xt_done, stat3, agg3, ve3, rs3, xn3_done, xo_done,
         t3_done, xn3t_done, kvd_done, kvdt_done, kvt_done, kva_done, qk_done, qksel_done, k_done, krope_a,
         krope_done, kr_done, q_done, qrope_a, qrope_done, qr_done, s_done, ttr_done, exp_done, tp_done, pte_done,
         pv_done, rec_done, norm_done, yt_done, yte_done, o_done, x4_done, stat4, agg4, ve4, rs4, xn4_done,
         t4_done, xn4t_done, qst_done, ms_done, s0_done, mx_done, mr_done, eq_done, eo_done, mask_done,
         g_done, u_done, gelu_done, inter_done, dn_done, fo_done, out_done) = (sems[n] for n in names)
        x_in = [sem(f"x3_in{c}") for c in range(NCH)]
        wq_in = [sem(f"wq_in{j}") for j in range(4)]
        wst_in = [sem(f"wst_in{j}") for j in range(4)]

        acc_v = [x.rearrange("(b t p) d -> b p t d", t=TT, p=P) for x in acc]
        out_v = out.rearrange("b (t p) d -> b p t d", p=P)
        PARTS4 = ((0, 0, TT - 1), (1, TT - 1, TT))
        N_W = 16

        def one(ap):
            return ap.rearrange("o p t d -> (o p) t d")

        def quads(eng, step):
            with eng.Fori(0, 3) as g:
                for j in range(4):
                    step(g, j)
            for j in range(4):
                step(3, j)

        def alone(eng):
            eng.nop(nofuse=True)

        def query_bank(g, j):
            return bs[j] if isinstance(g, int) and g == 0 and j < 2 else bq_[j % 2]

        def final(g, j):
            return isinstance(g, int) and g == 3 and j == 3

        def following(g, j):
            return None if final(g, j) else (g + (j + 1) // 4, (j + 1) % 4)

        def tiles():
            return [(o, TT - 1 - o) for o in range(TT)]

        block = nc.Block()
        block.__enter__()

        @block.sync
        def _(sy):
            for dst, src in ((wq[:], a["wq"].rearrange("(c p) n -> p c n", p=P)),
                             (wqsel[:], a["wqsel"].rearrange("(c p) n -> p c n", p=P)),
                             (wkd[:], a["L1_attn_Wkd"].rearrange("(c p) n -> p c n", p=P)),
                             (wkk[0:LAT], a["wkk"].rearrange("l (g n) -> l g n", g=NKV)),
                             (wksel[0:LAT], a["wksel"]),
                             (bq[:], a["bq"]), (bk[:], a["bk"]), (bkd[0:LAT], a["bkd"]),
                             (bqsel[0:SELD], a["bqsel"]), (bksel[0:SELD], a["bksel"]),
                             (rcos[:], a["rcos"]), (rsin[:], a["rsin"]),
                             (wo_sb, a["L1_attn_Wo"].rearrange("(h p) d -> p h d", p=P)),
                             (wvt_sb, a["wvt"]),
                             (bo_sb, a["L1_attn_bo"].partition_broadcast(P)), (bv_sb[:], a["bv"])):
                sy.dma_start(dst, src).then_inc(w3_in, 16)

            def load_x(b):
                if not isinstance(b, int):
                    sy.wait_ge(xo_done, b)
                    sy.wait_ge(xn3_done, b)
                for c in range(NCH):
                    sy.dma_start(xin[c][:], one(acc_v[c][ds(b, 1)])).then_inc(x_in[c], 16)

            def stage_q(g, j):
                sy.dma_start(wqs[:, j], wq[:, :, ds((g * 4 + j) * HD, HD)]).then_inc(wq_in[j], 16)

            def stage_ffn(g, j):
                for w in range(2):
                    sy.dma_start(wst[:, j, w], wffn[:, :, ds(w * FN + (g * 4 + j) * P, P)]).then_inc(wst_in[j], 16)

            load_x(0)
            for j in range(4):
                stage_ffn(0, j)
            sy.wait_ge(w3_in, 16 * N_W)
            for j in range(4):
                stage_q(0, j)

            def sequence(b, more):
                if more:
                    load_x(b + 1)
                with sy.Fori(0, 3) as g:
                    for j in range(4):
                        sy.wait_ge(q_done, b * 16 + g * 4 + j + 1)
                        stage_q(g + 1, j)
                if more:
                    for j in range(4):
                        sy.wait_ge(q_done, b * 16 + 12 + j + 1)
                        stage_q(0, j)
                with sy.Fori(0, 3) as g:
                    for j in range(4):
                        sy.wait_ge(u_done, b * 16 + g * 4 + j + 1)
                        stage_ffn(g + 1, j)
                if more:
                    for j in range(4):
                        sy.wait_ge(u_done, b * 16 + 12 + j + 1)
                        stage_ffn(0, j)
                sy.wait_ge(fo_done, b * 2 + 2 + 2)
                sy.dma_start(one(out_v[ds(b, 1)]), ob[:]).then_inc(out_done, 16)

            with sy.Fori(0, NB - 1) as b:
                sequence(b, True)
            sequence(NB - 1, False)
            sy.wait_ge(out_done, 16 * (NB + 1))

        @block.gpsimd
        def _(po):
            po.memset(ident[:], 0.0).then_inc(c0, 1)
            po.memset(causal[:], 0.0).then_inc(c0, 1)
            po.memset(offdiag[:], NEG).then_inc(c0, 1)
            po.memset(half_neg[:], -0.5).then_inc(c0, 1)
            po.memset(zero_w[:], 0.0).then_inc(c0, 1)
            po.memset(zero_m[:], 0.0).then_inc(c0, 1)
            po.memset(kva[:], 1.0).then_inc(c0, 1)
            po.wait_ge(c0, 7)
            po.affine_select(out=ident[:], in_=ident[:], compare_op=ALU.not_equal, fill=1.0, base=0,
                             pattern=[[-1, P]], channel_multiplier=1).then_inc(c3, 1)
            po.affine_select(out=causal[:], in_=causal[:], compare_op=ALU.is_ge, fill=NEG, base=(TT - 1) * P,
                             pattern=[[-1, WIDE]], channel_multiplier=1).then_inc(c3, 1)
            po.affine_select(out=offdiag[:], in_=offdiag[:], compare_op=ALU.not_equal, fill=0.0,
                             base=(TT - 1) * P, pattern=[[-1, WIDE]], channel_multiplier=1).then_inc(c3, 1)
            po.sem_inc(qr_done, 1)
            po.sem_inc(kr_done, 1)

            def first_norm(b):
                po.wait_ge(ve3, b + 1)
                po.tensor_tensor(rstd3[:], veps3[:], half_neg[:], ALU.pow).then_inc(rs3, 1)

            def keys(b, g):
                po.wait_ge(krope_done, b * 4 + g + 1 + 2)
                po.tensor_tensor(kr[:, g], ka[:], kb[:], ALU.add).then_inc(kr_done, 1)

            def residual(b):
                po.wait_ge(x4_done, b * 4 + 2)
                po.wait_ge(xs_done, b + 2)
                po.tensor_tensor(xo[:], xs[:], obias[:].unsqueeze(1).broadcast_to([P, TT, D]), ALU.add)\
                    .then_inc(xo_done, 1)

            def rotate(b, g, j):
                c = g * 4 + j
                po.wait_ge(qrope_done, b * 16 + c + 1 + 2)
                po.tensor_tensor(qr[:, j], qa[:], qb[:], ALU.add).then_inc(qr_done, 1)

            def attention(b):
                with po.Fori(0, 4) as g:
                    for j in range(4):
                        rotate(b, g, j)

            def second_norm(b):
                for part, lo, hi in PARTS4:
                    po.wait_ge(ve4, b * 2 + part + 1)
                    po.tensor_tensor(rstd4[:, lo:hi], veps4[:, lo:hi], half_neg[:, lo:hi], ALU.pow).then_inc(rs4, 1)

            po.wait_ge(obias_done, 1)
            first_norm(0)
            for g in range(NKV):
                keys(0, g)
            residual(0)
            with po.Fori(0, NB - 1) as b:
                attention(b)
                first_norm(b + 1)
                for g in range(NKV):
                    keys(b + 1, g)
                second_norm(b)
                residual(b + 1)
            attention(NB - 1)
            second_norm(NB - 1)

        @block.scalar
        def _(ac):
            ac.sem_inc(exp_done, 2)
            ac.sem_inc(pte_done, 2)
            ac.sem_inc(yte_done, 2)
            ac.sem_inc(gelu_done, 2)
            ac.wait_ge(w3_in, 16 * N_W)
            for hp in range(NH // 2):
                ac.wait_ge(wvt_done, hp + 1)
                ac.copy(wvo[0:LAT, hp], bs[hp % 2][0:LAT, 0:D])
                ac.copy(wvo[LAT:P, hp], bs[hp % 2][0:LAT, D:2 * D]).then_inc(wvo_done, 1)

            def front(b):
                for c in range(DC):
                    ac.wait_ge(t3_done, b * 2 + c + 1)
                    ac.copy(xn3t[:, c], bq_[c][:]).then_inc(xn3t_done, 1)

            def latents(b):
                ac.wait_ge(kvd_done, b + 1)
                ac.activation(kvdt[0:LAT], by[0][0:LAT, :], ACT.Identity, bias=bkd[0:LAT]).then_inc(kvdt_done, 1)

            def selectors(b):
                ac.wait_ge(qk_done, b + 1)
                ac.activation(qsel[0:SELD], bq_[0][0:SELD, :], ACT.Identity, bias=bqsel[0:SELD]).then_inc(qksel_done, 1)
                ac.activation(ksel[0:SELD], bq_[1][0:SELD, :], ACT.Identity, bias=bksel[0:SELD]).then_inc(qksel_done, 1)
                ac.wait_ge(kvt_done, b + 1)
                ac.copy(kva[:, :, 0:LAT], by[1][:, 0:TT * LAT].rearrange("p (t l) -> p t l", l=LAT)).then_inc(kva_done, 1)

            def select_query(b, o):
                ac.wait_ge(ms_done, b * 4 + o + 1)
                ac.wait_ge(qksel_done, b * 2 + 2)
                ac.copy(qst[0:SELD], qsel[0:SELD, ds((TT - 1) * P - o * P, P)]).then_inc(qst_done, 1)

            def exponents(b, g, j, o):
                t = TT - 1 - o
                n = (t + 1) * P
                ac.wait_ge(ttr_done, (b * 16 + g * 4 + j) * 4 + o + 1 + 2)
                ac.activation(pr[:, t, 0:n], sm[:, o % 2, 0:n], ACT.Exp, bias=nm[:, o % 2], scale=-1.0)\
                    .then_inc(exp_done, 1)

            def head(b, g, j, more):
                k = (b * 16 + g * 4 + j) * 4
                if final(g, j) and more:
                    front(b + 1)
                for o, t in tiles():
                    n = (t + 1) * P
                    ac.wait_ge(tp_done, k + o + 1)
                    ac.wait_ge(pv_done, k + o + 1)
                    ac.copy(pt[:, o % 2, 0:n], bp[o % 2][:, 0:n]).then_inc(pte_done, 1)
                    if o > 0 and following(g, j):
                        exponents(b, *following(g, j), o - 1)
                    if o == 1 and final(g, j) and more:
                        latents(b + 1)
                if following(g, j):
                    exponents(b, *following(g, j), TT - 1)

            def turned(b, t):
                for half in range(2):
                    ac.wait_ge(yt_done, b * 8 + t * 2 + half + 1)
                    ac.wait_ge(o_done, b * 4 + t + 1)
                    ac.copy(yt[:, t % 2, half * 4:half * 4 + 4].rearrange("p c q -> p (c q)"), bp[half][:])\
                        .then_inc(yte_done, 1)

            def turned4(b):
                for c in range(2):
                    ac.wait_ge(t4_done, b * 2 + c + 1)
                    ac.copy(xn4t[:, c], bp[c][:]).then_inc(xn4t_done, 1)

            def gelu(b, g, j):
                f = b * 16 + g * 4 + j
                ac.wait_ge(g_done, f + 1)
                ac.wait_ge(inter_done, f + 1)
                ac.activation(gl[:, j % 2], bq_[j % 2][:], ACT.Gelu_apprx_tanh).then_inc(gelu_done, 1)

            front(0)
            latents(0)
            selectors(0)
            with ac.Fori(0, TT) as i:
                select_query(0, i)

            def sequence(b, more):
                for o in range(TT):
                    exponents(b, 0, 0, o)
                quads(ac, lambda g, j: head(b, g, j, more))
                turned(b, 0)
                turned(b, 1)
                if more:
                    selectors(b + 1)
                turned(b, 2)
                turned(b, 3)
                if more:
                    select_query(b + 1, 0)
                turned4(b)

                def chunk(g, j):
                    gelu(b, g, j)
                    if j == 2 and more and not (isinstance(g, int) and g == 3):
                        select_query(b + 1, g + 1)

                quads(ac, chunk)

            with ac.Fori(0, NB - 1) as b:
                sequence(b, True)
            sequence(NB - 1, False)

        @block.tensor
        def _(pe):
            pe.sem_inc(pv_done, 2)
            pe.sem_inc(o_done, 2)
            pe.sem_inc(ms_done, 1)
            pe.sem_inc(dn_done, 2)
            pe.wait_ge(w3_in, 16 * N_W)
            pe.wait_ge(c3, 3)
            for hp in range(NH // 2):
                if hp >= 2:
                    pe.wait_ge(wvo_done, hp - 1)
                for i in range(2):
                    h = hp * 2 + i
                    mm = pe.matmul(bs[hp % 2][0:LAT, i * D:(i + 1) * D], wvt_sb[:, h // G], wo_sb[:, h],
                                   start=(i == 0), stop=True, skip_group_check=True)
                mm.then_inc(wvt_done, 1)
            pe.wait_ge(ob_ready, NKV)
            for h in range(NH):
                mm = pe.matmul(bp[0][:, 0:D], bvb[:, h // G], wo_sb[:, h], start=(h == 0), stop=(h == NH - 1))
            mm.then_inc(ob_ready, 1)

            def front(b):
                pe.wait_ge(xn3_done, b + 1)
                for c in range(DC):
                    for t in range(TT):
                        mm = pe.transpose(bq_[c][:, t * P:(t + 1) * P], xn3[:, t, c * P:(c + 1) * P], ident[:])
                    mm.then_inc(t3_done, 1)

            def latents(b):
                pe.wait_ge(xn3t_done, b * 2 + 2)
                alone(pe)
                for c in range(DC):
                    mm = pe.matmul(by[0][0:LAT, :], wkd[:, c], xn3t[:, c], start=(c == 0), stop=(c == DC - 1))
                mm.then_inc(kvd_done, 1)

            def selectors(b):
                for c in range(DC):
                    pe.matmul(bq_[0][0:SELD, :], wqsel[:, c], xn3t[:, c], start=(c == 0), stop=(c == DC - 1))
                pe.wait_ge(kvdt_done, b + 1)
                alone(pe)
                pe.matmul(bq_[1][0:SELD, :], wksel[0:LAT], kvdt[0:LAT], start=True, stop=True).then_inc(qk_done, 1)
                for t in range(TT):
                    mm = pe.transpose(by[1][:, t * LAT:(t + 1) * LAT], kvdt[0:LAT, t * P:(t + 1) * P], ident[0:LAT, 0:LAT])
                mm.then_inc(kvt_done, 1)

            def keys(b, g):
                pe.wait_ge(qksel_done, b * 2 + 2)
                pe.wait_ge(krope_done, b * 4 + g + 1)
                alone(pe)
                pe.matmul(bq_[g % 2][:], wkk[0:LAT, g], kvdt[0:LAT], start=True, stop=True).then_inc(k_done, 1)

            def select_scores(b, i):
                pe.wait_ge(qst_done, b * 4 + i + 1)
                pe.wait_ge(s0_done, b * 4 + i + 1)
                pe.wait_ge(qrope_done, b * 16 + 1 + 2)
                alone(pe)
                pe.matmul(bs[0][:], qst[0:SELD], ksel[0:SELD], start=True, stop=True).then_inc(ms_done, 1)

            def query(b, g, j):
                m = b * 16 + g * 4 + j
                pe.wait_ge(wq_in[j], (b * 4 + g) * 16 + 16)
                pe.wait_ge(qrope_done, m + 1)
                for c in range(DC):
                    mm = pe.matmul(query_bank(g, j)[:], wqs[:, j, c], xn3t[:, c], start=(c == 0), stop=(c == DC - 1))
                mm.then_inc(q_done, 1)

            def scores(b, g, j, o):
                t = TT - 1 - o
                m = b * 16 + g * 4 + j
                n = (t + 1) * P
                if o == 0:
                    pe.wait_ge(qr_done, m + 1 + 1)
                pe.wait_ge(ttr_done, m * 4 + o + 1)
                pe.matmul(bs[o % 2][:, 0:n], qr[:, j, t * P:(t + 1) * P],
                          kr[:, ds(g, 1), 0:n].rearrange("p o n -> p (o n)"), start=True, stop=True)\
                    .then_inc(s_done, 1)

            def head(b, g, j, more):
                m = b * 16 + g * 4 + j
                k = m * 4

                def transpose(o, t):
                    pe.wait_ge(exp_done, k + o + 1 + 2)
                    pe.wait_ge(pte_done, k + o + 1)
                    for i in range(t + 1):
                        mm = pe.transpose(bp[o % 2][:, i * P:(i + 1) * P], pr[:, t, i * P:(i + 1) * P], ident[:])
                    mm.then_inc(tp_done, 1)

                def values(o, t):
                    if o == 0:
                        pe.wait_ge(norm_done, m + 1)
                    pe.wait_ge(pte_done, k + o + 1 + 2)
                    for i in range(t + 1):
                        mm = pe.matmul(by[j % 2][:, t * AUG:(t + 1) * AUG], pt[:, o % 2, i * P:(i + 1) * P], kva[:, i],
                                       start=(o == 0 and i == 0), stop=(i == t), skip_group_check=True)
                    mm.then_inc(pv_done, 1)

                if not (isinstance(g, int) and g == 3 and j >= 2):
                    query(b, g + (j + 2) // 4, (j + 2) % 4)
                if final(g, j) and more:
                    front(b + 1)
                for o, t in tiles():
                    transpose(o, t)
                    if following(g, j):
                        scores(b, *following(g, j), o)
                    if o > 0:
                        values(*tiles()[o - 1])
                    if o == 1 and final(g, j) and more:
                        pe.wait_ge(norm_done, m + 2)
                        latents(b + 1)
                values(*tiles()[TT - 1])

            def turn(b, t):
                for half in range(2):
                    pe.wait_ge(yte_done, b * 8 + t * 2 + half + 1)
                    for c in range(4):
                        hp = half * 4 + c
                        mm = pe.transpose(bp[half][:, c * P:(c + 1) * P],
                                          ym[:, t, hp * 2:hp * 2 + 2].rearrange("p h l -> p (h l)"), ident[:])
                    mm.then_inc(yt_done, 1)

            def project(b, t):
                pe.wait_ge(yte_done, b * 8 + t * 2 + 2 + 2)
                pe.wait_ge(x4_done, b * 4 + t + 1)
                for hp in range(NH // 2):
                    mm = pe.matmul(bs[t % 2][:, 0:D], yt[:, t % 2, hp], wvo[:, hp], start=(hp == 0),
                                   stop=(hp == NH // 2 - 1))
                mm.then_inc(o_done, 1)

            def output(b, more):
                pe.wait_ge(norm_done, b * 16 + 16 + 2)
                turn(b, 0)
                turn(b, 1)
                if more:
                    selectors(b + 1)
                for t in range(TT):
                    project(b, t)
                    if more:
                        keys(b + 1, t)
                    if t + 2 < TT:
                        turn(b, t + 2)
                for part, lo, hi in PARTS4:
                    if more:
                        pe.wait_ge(x4_done, b * 4 + part + 3 + 2)
                        alone(pe)
                        query(b + 1, 0, part)
                    turn4(b, part, lo, hi)
                pe.wait_ge(xn4t_done, b * 2 + 2)
                for c in range(2):
                    pe.matmul(bp[c][:], zero_w[:], zero_m[:], start=True, stop=False, skip_group_check=True)

            def turn4(b, part, lo, hi):
                pe.wait_ge(xn4_done, b * 2 + part + 1)
                for c in range(2):
                    for t in range(lo, hi):
                        mm = pe.transpose(bp[c][:, t * P:(t + 1) * P], xn4[:, t, c::2], ident[:])
                    if part == 1:
                        mm.then_inc(t4_done, 1)

            def gate_up(b, g, j):
                f = b * 16 + g * 4 + j
                pe.wait_ge(wst_in[j], (b * 4 + g) * 32 + 32)
                pe.wait_ge(gelu_done, f + 1)
                pe.wait_ge(inter_done, f + 1)
                for w, banks, done in ((0, bq_, g_done), (1, by, u_done)):
                    for c in range(2):
                        mm = pe.matmul(banks[j % 2][:], wst[:, j, w, c], xn4t[:, c], start=(c == 0), stop=(c == 1))
                    mm.then_inc(done, 1)

            def down(b, g, j):
                f = b * 16 + g * 4 + j
                pe.wait_ge(inter_done, f + 1 + 2)
                at = 2 * FN + (g * 2 + j // 2) * D
                for t in range(TT):
                    mm = pe.matmul(bp[t // 2][:, (t % 2) * D:(t % 2 + 1) * D], it[:, j % 2, t * P:(t + 1) * P],
                                   wffn[:, j % 2, ds(at, D)], start=False, stop=False, skip_group_check=True)
                mm.then_inc(dn_done, 1)

            pe.wait_ge(obias_done, 1)
            front(0)
            latents(0)
            selectors(0)
            for g in range(NKV):
                keys(0, g)
            query(0, 0, 0)
            query(0, 0, 1)
            with pe.Fori(0, TT) as i:
                select_scores(0, i)

            def sequence(b, more):
                alone(pe)
                pe.wait_ge(kr_done, b * 4 + 4 + 1)
                pe.wait_ge(kva_done, b + 1)
                pe.wait_ge(s0_done, b * 4 + 4 + 1)
                for o in range(TT):
                    if o == 1:
                        pe.wait_ge(qrope_done, b * 16 + 2 + 2)
                    scores(b, 0, 0, o)
                pe.wait_ge(fo_done, b * 2 + 2)
                alone(pe)
                quads(pe, lambda g, j: head(b, g, j, more))
                output(b, more)
                if more:
                    pe.wait_ge(krope_done, b * 4 + 4 + 4 + 2)
                    pe.wait_ge(qksel_done, b * 2 + 4)
                    pe.wait_ge(kva_done, b + 2)
                gate_up(b, 0, 0)

                def chunk(g, j):
                    if j == 0 and more:
                        select_scores(b + 1, g)
                    if not (isinstance(g, int) and g == 3 and j == 3):
                        gate_up(b, g + (j + 1) // 4, (j + 1) % 4)
                    down(b, g, j)

                quads(pe, chunk)

            with pe.Fori(0, NB - 1) as b:
                sequence(b, True)
            sequence(NB - 1, False)

        @block.vector
        def _(ve):
            ve.sem_inc(xs_done, 1)
            ve.sem_inc(x4_done, 2)
            ve.sem_inc(krope_done, 2)
            ve.sem_inc(qrope_done, 2)
            ve.sem_inc(ttr_done, 2)
            ve.sem_inc(norm_done, 2)
            ve.sem_inc(s0_done, 1)
            ve.sem_inc(inter_done, 2)
            ve.sem_inc(fo_done, 2)
            ve.sem_inc(out_done, 16)
            ve.wait_ge(c3, 3)
            ve.wait_ge(w3_in, 16 * N_W)
            for g in range(NKV):
                ve.tensor_copy(bvb[:, g], bv_sb[:, g:g + 1].broadcast_to([P, P])).then_inc(ob_ready, 1)
            ve.wait_ge(ob_ready, NKV + 1)
            ve.tensor_tensor(obias[:], bp[0][:, 0:D], bo_sb, ALU.add)\
                .then_inc(obias_done, 1)

            def sum_stats(b, t):
                if t == 0:
                    for c in range(NCH):
                        ve.wait_ge(x_in[c], b * 16 + 16)
                ins = ve.tensor_tensor(xs[:, t], xin[0][:, t], xin[1][:, t], ALU.add)
                ins.then_inc(xt_done, 1)
                ve.wait_ge(xt_done, b * 4 + t + 1)
                if t == TT - 1:
                    ve.sem_inc(xs_done, 1)
                ve.bn_stats(bnbuf[:, t], xs[:, t]).then_inc(stat3, 1)
                ve.wait_ge(stat3, b * 4 + t + 1)
                alone(ve)
                ve.bn_aggr(mv3[:, t], bnbuf[:, t]).then_inc(agg3, 1)

            def first_norm(b):
                ve.wait_ge(agg3, b * 4 + 4)
                ve.tensor_scalar(veps3[:], mv3[:, :, 1], EPS, None, ALU.add).then_inc(ve3, 1)

            def first_scale(b):
                ve.wait_ge(rs3, b + 1)
                for t in range(TT):
                    ins = ve.tensor_scalar(xn3[:, t], xs[:, t], mv3[:, t, 0:1], rstd3[:, t:t + 1], ALU.subtract, ALU.mult)
                ins.then_inc(xn3_done, 1)

            def rotary(src, bias, ta, tb, done_a, done, n):
                ve.scalar_tensor_tensor(out=ta[:], in0=src[:], scalar=bias(0, P), in1=rcos[:], op0=ALU.add, op1=ALU.mult)\
                    .then_inc(done_a, 1)
                ve.scalar_tensor_tensor(out=tb[H2:P], in0=src[0:H2], scalar=bias(0, H2), in1=rsin[0:H2], op0=ALU.add,
                                        op1=ALU.mult).then_inc(done_a, 1)
                ve.scalar_tensor_tensor(out=tb[0:H2], in0=src[H2:P], scalar=bias(H2, P), in1=rsin[H2:P], op0=ALU.add,
                                        op1=ALU.mult).then_inc(done, 1)

            def keys(b, *groups):
                for g in groups:
                    n = b * 4 + g
                    ve.wait_ge(k_done, n + 1)
                    ve.wait_ge(kr_done, n + 1)
                    rotary(bq_[g % 2], lambda lo, hi: bk[lo:hi, g:g + 1], ka, kb, krope_a, krope_done, n)

            def query(b, g, j):
                n = b * 16 + g * 4 + j
                ve.wait_ge(q_done, n + 1)
                ve.wait_ge(qr_done, n + 1)
                if query_bank(g, j) is bs[0]:
                    ve.wait_ge(kr_done, b * 4 + 4 + 1)
                rotary(query_bank(g, j), lambda lo, hi: bq[lo:hi, ds(g * 4 + j, 1)], qa, qb, qrope_a, qrope_done, n)

            def masked(b, g, j, o):
                k = (b * 16 + g * 4 + j) * 4
                t = TT - 1 - o
                n = (t + 1) * P
                ve.wait_ge(s_done, k + o + 1)
                ve.wait_ge(exp_done, k + o + 1)
                alone(ve)
                ve.tensor_tensor_reduce(sm[:, o % 2, 0:n], bs[o % 2][:, 0:n], mask[:, t, 0:n], -QS, 3.0e38,
                                        ALU.add, ALU.min, nm[:, o % 2]).then_inc(ttr_done, 1)

            def head(b, g, j):
                m = b * 16 + g * 4 + j
                k = m * 4
                if not (isinstance(g, int) and g == 3 and j >= 2):
                    query(b, g + (j + 2) // 4, (j + 2) % 4)
                for o in range(TT):
                    if following(g, j):
                        masked(b, *following(g, j), o)
                ve.wait_ge(pv_done, k + 4 + 2)
                y = by[j % 2][:, 0:TT * AUG].rearrange("p (t l) -> p t l", l=AUG)
                ve.wait_ge(norm_done, m + 2)
                ve.reciprocal(rec[:], y[:, :, LAT]).then_inc(rec_done, 1)
                ve.wait_ge(rec_done, m + 1)
                ve.tensor_tensor(ym[:, :, ds(g * 4 + j, 1)].rearrange("p t o l -> p t (o l)"), y[:, :, 0:LAT],
                                 rec[:].unsqueeze(2).broadcast_to([P, TT, LAT]), ALU.mult).then_inc(norm_done, 1)

            def residual(b, t):
                if t == 0:
                    ve.wait_ge(xo_done, b + 1)
                ve.wait_ge(o_done, b * 4 + t + 1 + 2)
                ve.tensor_tensor(x4[:, t], bs[t % 2][:, 0:D], xo[:, t], ALU.add).then_inc(x4_done, 1)
                ve.wait_ge(x4_done, b * 4 + t + 1 + 2)
                ve.bn_stats(bnbuf4[:, t], x4[:, t]).then_inc(stat4, 1)
                ve.wait_ge(stat4, b * 4 + t + 1)
                alone(ve)
                ve.bn_aggr(mv4[:, t], bnbuf4[:, t]).then_inc(agg4, 1)

            def second_norm(b, part, lo, hi):
                ve.wait_ge(agg4, b * 4 + hi)
                ve.tensor_scalar(veps4[:, lo:hi], mv4[:, lo:hi, 1], EPS, None, ALU.add).then_inc(ve4, 1)

            def second_scale(b, part, lo, hi):
                ve.wait_ge(rs4, b * 2 + part + 1)
                ve.wait_ge(out_done, b * 16 + 16)
                for t in range(lo, hi):
                    ins = ve.tensor_scalar(xn4[:, t], x4[:, t], mv4[:, t, 0:1], rstd4[:, t:t + 1], ALU.subtract, ALU.mult)
                ins.then_inc(xn4_done, 1)

            def select_start(b, o):
                n = (TT - o) * P
                ve.wait_ge(ms_done, b * 4 + o + 1 + 1)
                ve.tensor_tensor(s0[:, 0:n], bs[0][:, 0:n], causal[:, o * P:o * P + n], ALU.add).then_inc(s0_done, 1)

            def select_round(b, o, r):
                n = (b * 4 + o) * (SELK // 8) + r
                w = (TT - o) * P
                src = s0[:, 0:w] if r == 0 else sr[:, (r - 1) % 2, 0:w]
                if r == 0:
                    ve.wait_ge(s0_done, b * 4 + o + 1 + 1)
                else:
                    ve.wait_ge(mr_done, n)
                alone(ve)
                ve.max(m8[:], src).then_inc(mx_done, 1)
                ve.wait_ge(mx_done, n + 1)
                alone(ve)
                ve.match_replace(sr[:, r % 2, 0:w], m8[:], src, GONE).then_inc(mr_done, 1)

            def select_end(b, o):
                n = b * 4 + o + 1
                w = (TT - o) * P
                ve.wait_ge(mr_done, n * (SELK // 8))
                ve.tensor_tensor(eq[:, 0:w], sr[:, (SELK // 8 - 1) % 2, 0:w], s0[:, 0:w], ALU.is_equal).then_inc(eq_done, 1)
                ve.wait_ge(eq_done, n)
                ve.tensor_tensor(eo[:, 0:w], eq[:, 0:w], offdiag[:, o * P:o * P + w], ALU.mult).then_inc(eo_done, 1)
                ve.wait_ge(eo_done, n)
                ve.tensor_tensor(mask[:, TT - 1 - o, 0:w], eo[:, 0:w], causal[:, o * P:o * P + w], ALU.add)\
                    .then_inc(mask_done, 1)

            def hidden(b, g, j):
                f = b * 16 + g * 4 + j
                ve.wait_ge(u_done, f + 1)
                ve.wait_ge(gelu_done, f + 1 + 2)
                ve.wait_ge(dn_done, f + 1)
                ve.tensor_tensor(it[:, j % 2], by[j % 2][:], gl[:, j % 2], ALU.mult).then_inc(inter_done, 1)

            for t in range(TT):
                sum_stats(0, t)
            first_norm(0)
            first_scale(0)
            keys(0, *range(NKV))
            query(0, 0, 0)
            query(0, 0, 1)
            for o in range(TT):
                select_start(0, o)
                for r in range(SELK // 8):
                    select_round(0, o, r)
                select_end(0, o)
            ve.wait_ge(mask_done, 4)
            for o in range(TT):
                masked(0, 0, 0, o)

            def sequence(b, more):
                def step(g, j):
                    if more and isinstance(g, int) and j == 3:
                        first_scale(b + 1)
                    head(b, g, j)
                    if more and isinstance(g, int) and j < 2:
                        sum_stats(b + 1, j * 2)
                        sum_stats(b + 1, j * 2 + 1)
                        if j == 1:
                            first_norm(b + 1)

                quads(ve, step)
                for t in range(TT):
                    residual(b, t)
                    for part, lo, hi in PARTS4:
                        if hi == t + 1:
                            second_norm(b, part, lo, hi)
                    if more and t < TT - 1:
                        keys(b + 1, t)
                    if more and t == TT - 2:
                        keys(b + 1, TT - 1)
                    if t >= TT - 2:
                        second_scale(b, *PARTS4[t - TT + 2])
                if more:
                    query(b + 1, 0, 0)
                    query(b + 1, 0, 1)

                rounds = ((0, 1), (2, 3), (4, 5), (6, 7))
                for g in range(4):
                    for j in range(4):
                        if j == 0 and more:
                            select_start(b + 1, g)
                        hidden(b, g, j)
                        if more:
                            for r in rounds[j]:
                                select_round(b + 1, g, r)
                            if j == 3:
                                select_end(b + 1, g)
                if more:
                    ve.wait_ge(mask_done, b * 4 + 4 + 4)
                    masked(b + 1, 0, 0, 0)
                    masked(b + 1, 0, 0, 1)
                ve.wait_ge(dn_done, b * 16 + 16 + 2)
                ve.wait_ge(out_done, b * 16 + 16)
                for half in range(2):
                    t0 = half * 2
                    ve.tensor_tensor(ob[:, t0:t0 + 2].rearrange("p t d -> p (t d)"), bp[half][:],
                                     x4[:, t0:t0 + 2].rearrange("p t d -> p (t d)"), ALU.add).then_inc(fo_done, 1)
                if more:
                    masked(b + 1, 0, 0, 2)
                    masked(b + 1, 0, 0, 3)

            with ve.Fori(0, NB - 1) as b:
                sequence(b, True)
            sequence(NB - 1, False)

        block.__exit__(None, None, None)
        sp.clear()


def lay_out(inputs):
    t = dict(inputs)
    a = {n: t[n] for n in ("L0_attn_x", "L0_attn_D_skip")}
    a["b_dt"] = t["L0_attn_b_dt"].reshape(DC, P).T
    a["a_log"] = t["L0_attn_A_log"].reshape(DC, P).T
    a["w_dt_t"] = t["L0_attn_W_dt"].T
    a["w_b_t"] = t["L0_attn_W_B"].T
    a["w_c_t"] = t["L0_attn_W_C"].T
    a["w_r_t"] = t["L0_ffn_router_weight"].T
    order = np.arange(FN).reshape(FN // 2 // P, P, 2).transpose(0, 2, 1).reshape(-1)
    jc = FN // 2 // P
    down = t["L1_ffn_down_W_packed"].T.reshape(jc, P, D).transpose(1, 0, 2).reshape(P, FN)
    a["codes"] = np.concatenate([t["L1_ffn_gate_W_packed"][order].T, t["L1_ffn_up_W_packed"][order].T, down], 1)
    down_s = t["L1_ffn_down_scales"].T.reshape(jc, P // 16, D).transpose(1, 0, 2).reshape(P // 16, FN)
    a["scales"] = np.concatenate([t["L1_ffn_gate_scales"][order].T, t["L1_ffn_up_scales"][order].T, down_s], 1)
    pair = np.concatenate([np.arange(0, HD, 2), np.arange(1, HD, 2)])
    wku, bku = t["L1_attn_Wku"], t["L1_attn_bku"]
    kd = NKV * HD
    a["wq"] = t["L1_attn_Wq"].reshape(D, NH, HD)[:, :, pair].reshape(D, NH * HD)
    a["wqsel"] = t["L1_attn_Wq"][:, :SELD]
    a["wkk"] = wku[:, :kd].reshape(LAT, NKV, HD)[:, :, pair].reshape(LAT, kd)
    a["wksel"] = wku[:, :SELD]
    a["wvt"] = wku[:, kd:].reshape(LAT, NKV, HD).transpose(2, 1, 0)
    a["bq"] = t["L1_attn_bq"].reshape(NH, HD)[:, pair].T
    a["bk"] = bku[:kd].reshape(NKV, HD)[:, pair].T
    a["bv"] = bku[kd:].reshape(NKV, HD).T
    a["bkd"] = t["L1_attn_bkd"][:, None]
    a["bqsel"] = t["L1_attn_bq"][:SELD, None]
    a["bksel"] = bku[:SELD, None]
    for n in ("L1_attn_Wkd", "L1_attn_Wo", "L1_attn_bo"):
        a[n] = t[n]
    inv = np.float32(1.0) / np.float32(10000.0) ** (np.arange(0, HD, 2, dtype=np.float32) / np.float32(HD))
    angle = np.arange(S, dtype=np.float32)[:, None] * inv[None, :]
    angle = np.concatenate([angle, angle], 1)[:, ::2].T.astype(np.float32)
    a["rcos"] = np.concatenate([np.cos(angle), np.cos(angle)], 0)
    a["rsin"] = np.concatenate([np.sin(angle), -np.sin(angle)], 0)
    a["L0_ffn_gate_up_proj"] = t["L0_ffn_gate_up_proj"]
    a["L0_ffn_down_proj"] = t["L0_ffn_down_proj"]
    return {n: np.ascontiguousarray(v) for n, v in a.items()}


def program(nc, a, out):
    acc = [nc.dram_tensor(f"acc{c}", (T, D), F32, kind="Internal").ap() for c in range(NCH)]
    xg = nc.dram_tensor("rows_for_experts", (T, ROW), F32, kind="Internal").ap()
    with ExitStack() as st:
        sb = Space(nc, st).sb
        slots = sb("slots", [P, NE, 2], I32)
        stage1(nc, a, acc, xg, slots)
        wffn = sb("wffn", [P, 2, 3 * FN])
        stage2(nc, a, acc, xg, slots, wffn)
        stage3(nc, a, acc, wffn, out)


def kernel(**inputs):
    import concourse.bacc as bacc
    from concourse.bass_utils import run_bass_kernel_spmd

    arrays = lay_out({n: np.asarray(v) for n, v in inputs.items()})
    nc = bacc.Bacc("TRN2", target_bir_lowering=False, num_devices=1)
    a = {n: nc.dram_tensor(f"in_{n}", v.shape, mybir.dt.from_np(v.dtype), kind="ExternalInput").ap()
         for n, v in arrays.items()}
    out = nc.dram_tensor("out", (NB, S, D), F32, kind="ExternalOutput").ap()
    program(nc, a, out)
    r = run_bass_kernel_spmd(nc, [{f"in_{n}": v for n, v in arrays.items()}], core_ids=[0])
    return r.results[0]["out"]
```

```python
from contextlib import ExitStack

import numpy as np

import concourse.bass as bass
from concourse import mybir

F32 = mybir.dt.float32
BF16 = mybir.dt.bfloat16
F16 = mybir.dt.float16
F32R = mybir.dt.float32r
I32 = mybir.dt.int32
ALU = mybir.AluOpType
ACT = mybir.ActivationFunctionType
AX = mybir.AxisListType
ds = bass.ds

P = 128
NB, S, D = 8, 512, 256
T = NB * S
TT = S // P
DC = D // P
EPS = 1e-5

NE, TOPK, CAP, FF = 64, 8, 128, 96
HI, LO = 16, 8
EG = NE // LO
ROW = D + NE
NCH = 2

NH, HD, NKV, LAT, SELD, SELK = 16, 128, 4, 64, 64, 64
G = NH // NKV
NEG = -1.0e30
GONE = -3.0e38
FN = 2048
FNC = FN // P


class Space:

    def __init__(self, nc, stack, stage=""):
        self.nc, self.stack, self.stage = nc, stack, stage
        self.sems = []

    def sb(self, name, shape, dt=F32):
        return self.stack.enter_context(self.nc.sbuf_tensor(name, shape, dt))

    def banks(self, name, n=1):
        return [self.stack.enter_context(self.nc.psum_tensor(f"{name}{i}", [P, 512], F32)) for i in range(n)]

    def sem(self, name):
        self.sems.append(self.nc.alloc_semaphore(name=self.stage + name))
        return self.sems[-1]

    def clear(self):
        self.nc.clear_and_free_semaphores(self.sems)
        self.nc.all_engine_barrier()


def stage1(nc, a, acc, xg, slots, codes, scales):
    xa = acc[0]
    with ExitStack() as st:
        sp = Space(nc, st, "s1_")
        sb, sem = sp.sb, sp.sem
        ident = sb("ident", [P, P])
        w_dt = sb("w_dt", [P, DC, D])
        w_b = sb("w_b", [P, DC, D])
        w_c = sb("w_c", [P, DC, D])
        w_r = sb("w_r", [P, DC, NE])
        b_dt = sb("b_dt", [P, DC])
        a_log = sb("a_log", [P, DC])
        a_exp = sb("a_exp", [P, DC])
        a_neg = sb("a_neg", [P, DC])
        dskip = sb("dskip", [P, D])
        half_neg = sb("half_neg", [P, TT])
        upto = sb("upto", [P, P], BF16)
        ones = sb("ones", [P, P], BF16)
        iota_hi = sb("iota_hi", [P, HI, NE], BF16)
        iota_lo = sb("iota_lo", [P, LO, NE], BF16)
        blank = sb("blank", [P, D])
        row1 = sb("row1", [P, 1])
        tile_no = sb("tile_no", [P, T // P])
        same_e = sb("same_e", [P, LO])
        same_hi = sb("same_hi", [P, HI])
        spread = sb("spread", [P, LO, HI, LO])
        xb = sb("xb", [P, 2, TT, D])
        xn = sb("xn", [P, 2, TT, D])
        xd = sb("xd", [P, 2, TT, D])
        stat = sb("stat", [P, TT, 6])
        mv = sb("mv", [P, TT, 2])
        veps = sb("veps", [P, TT])
        rstd = sb("rstd", [P, TT])
        xnt = sb("xnt", [P, DC, S])
        z = sb("z", [P, DC, S])
        az = sb("az", [P, DC, S])
        ez = sb("ez", [P, DC, S])
        lz = sb("lz", [P, DC, S])
        dt = sb("dt", [P, DC, S])
        abar = sb("abar", [P, DC, S])
        ub = sb("ub", [P, DC, S])
        ux = sb("ux", [P, DC, S])
        h = sb("h", [P, 2, DC, S])
        x1 = sb("x1", [P, TT, D])
        rows = sb("rows", [P, TT, ROW])
        stat2 = sb("stat2", [P, TT, 6])
        mv2 = sb("mv2", [P, TT, 2])
        veps2 = sb("veps2", [P, TT])
        rstd2 = sb("rstd2", [P, TT])
        xn2t = sb("xn2t", [P, DC, S])
        lg = sb("lg", [P, TT, NE])
        top8 = sb("top8", [P, TT, TOPK])
        lrest = sb("lrest", [P, TT, NE])
        sel = sb("sel", [P, TT, NE], BF16)
        ls = sb("ls", [P, TT, NE])
        el = sb("el", [P, TT, NE])
        es = sb("es", [P, TT, NE])
        esum = sb("esum", [P, TT])
        erec = sb("erec", [P, TT])
        bsum = sb("bsum", [P, NE])
        before = sb("before", [P, NE], BF16)
        before_f = sb("before_f", [P, NE])
        q0 = sb("q0", [P, TT, NE])
        qi = sb("qi", [P, TT, NE], I32)
        qh = sb("qh", [P, TT, NE], I32)
        ql = sb("ql", [P, TT, NE], I32)
        qhb = sb("qhb", [P, TT, NE], BF16)
        qlb = sb("qlb", [P, TT, NE], BF16)
        oh_hi = sb("oh_hi", [P, TT, HI, NE], BF16)
        oh_lo = sb("oh_lo", [P, LO, NE], BF16)
        oh_v = sb("oh_v", [P, TT, 2, LO, NE], BF16)
        slot_acc = sb("slot_acc", [P, EG, 2, LO, LO])
        slot_m = sb("slot_m", [P, EG, 2, LO, LO])
        tokf = sb("tokf", [P, 2, NE])
        tid = sb("tid", [P, NE])
        emp = sb("emp", [P, NE])
        gf = sb("gf", [P, NE])
        sf = sb("sf", [P, NE])

        bank_t = sp.banks("bank_t", 2)
        bank_d = sp.banks("bank_d", 2)
        bank_b = sp.banks("bank_b", 2)
        bank_o = sp.banks("bank_o", 2)

        consts_in = sem("consts_in")
        consts_pool = sem("consts_pool")
        x_in = [sem(f"x_in{u}") for u in range(2)]
        x_free = sem("x_free")
        rows_out = sem("rows_out")
        aexp_done = sem("aexp_done")
        aneg_done = sem("aneg_done")
        zeroed = sem("zeroed")
        stat_done = sem("stat_done")
        mv_done = sem("mv_done")
        veps_done = sem("veps_done")
        rstd_done = sem("rstd_done")
        xn_done = sem("xn_done")
        dx_done = sem("dx_done")
        xd_done = sem("xd_done")
        t_done = sem("t_done")
        xnt_done = sem("xnt_done")
        d_done = sem("d_done")
        b_done = sem("b_done")
        z_done = sem("z_done")
        az_done = sem("az_done")
        ez_done = sem("ez_done")
        lz_done = sem("lz_done")
        dt_done = sem("dt_done")
        abar_done = sem("abar_done")
        ub_done = sem("ub_done")
        ux_done = sem("ux_done")
        h_done = sem("h_done")
        o_done = sem("o_done")
        x1_done = sem("x1_done")
        stat2_done = sem("stat2_done")
        mv2_done = sem("mv2_done")
        veps2_done = sem("veps2_done")
        rstd2_done = sem("rstd2_done")
        xn2_done = sem("xn2_done")
        t2_done = sem("t2_done")
        xn2t_done = sem("xn2t_done")
        r_done = sem("r_done")
        lg_done = sem("lg_done")
        top_done = sem("top_done")
        lrest_done = sem("lrest_done")
        sel_done = sem("sel_done")
        ls_done = sem("ls_done")
        el_done = sem("el_done")
        es_done = sem("es_done")
        esum_done = sem("esum_done")
        erec_done = sem("erec_done")
        wts_done = sem("wts_done")
        pos_done = sem("pos_done")
        q0_done = sem("q0_done")
        bsum_done = sem("bsum_done")
        beforef_done = sem("beforef_done")
        before_done = sem("before_done")
        qi_done = sem("qi_done")
        qhl_done = sem("qhl_done")
        qb_done = sem("qb_done")
        hi_done = sem("hi_done")
        lo_done = sem("lo_done")
        v_done = sem("v_done")
        inv_done = sem("inv_done")
        acc_done = sem("acc_done")
        fin = sem("fin")
        fin_pe = sem("fin_pe")
        xa_out = sem("xa_out")
        acc_free = sem("acc_free")
        blank_done = sem("blank_done")
        blank_out = sem("blank_out")
        packed_in = sem("packed_in")
        q_free = sem("q_free")
        same_done = sem("same_done")

        block = nc.Block()
        block.__enter__()

        xa_v = xa.rearrange("(b t p) d -> b p t d", t=TT, p=P)
        xg_v = xg.rearrange("(b t p) d -> b p t d", t=TT, p=P)
        x_v = a["L0_attn_x"].rearrange("b (t p) d -> b p t d", p=P)

        def one(ap):
            return ap.rearrange("o p t d -> (o p) t d")

        def first(n):
            return isinstance(n, int) and n == 1

        def seq(i, u):
            return i * 2 + u

        def steps(eng, step):
            step(0, 1, 1, True, False)
            step(1, 0, 1, True, False)
            with eng.Fori(0, NB // 2 - 1) as i:
                for u in range(2):
                    step(seq(i, u) + 2, 1 - u, i + 2, True, True)
            step(NB, 1, NB // 2, False, True)
            step(NB + 1, 0, NB // 2, False, True)

        def middle(n):
            return not (isinstance(n, int) and n in (0, NB + 1))

        @block.sync
        def _(sy):
            for dst, src in ((w_dt, "w_dt_t"), (w_b, "w_b_t"), (w_c, "w_c_t"), (w_r, "w_r_t")):
                sy.dma_start(dst[:], a[src].rearrange("(c p) n -> p c n", p=P)).then_inc(consts_in, 16)
            for dst, src in ((b_dt, "b_dt"), (a_log, "a_log")):
                sy.dma_start(dst[:], a[src]).then_inc(consts_in, 16)
            sy.dma_start(dskip[:], a["L0_attn_D_skip"].partition_broadcast(P)).then_inc(consts_in, 16)
            with sy.Fori(0, NB // 2) as i:
                for u in range(2):
                    sy.wait_ge(x_free, seq(i, u) + 1)
                    sy.dma_start(xb[:, u], one(x_v[ds(seq(i, u), 1)])).then_inc(x_in[u], 16)
            sy.wait_ge(blank_done, 1)
            for other in acc[1:]:
                sy.dma_start(other.rearrange("(b p) d -> p b d", p=P),
                             blank[:].unsqueeze(1).broadcast_to([P, T // P, D])).then_inc(blank_out, 16)
            sy.dma_start(codes, a["codes"]).then_inc(packed_in, 16)
            for b in range(P // 16):
                sy.dma_start(scales[b * 16:(b + 1) * 16], a["scales"][b].partition_broadcast(16)).then_inc(packed_in, 16)
            sy.wait_ge(blank_out, 16 * (NCH - 1))
            sy.wait_ge(packed_in, 16 * (1 + P // 16))

        @block.gpsimd
        def _(po):
            po.sem_inc(x_free, 2)
            po.memset(blank[:], 0.0).then_inc(blank_done, 1)
            po.memset(ident[:], 0.0).then_inc(consts_pool, 1)
            po.memset(upto[:], 1.0).then_inc(consts_pool, 1)
            po.memset(ones[:], 1.0).then_inc(consts_pool, 1)
            po.memset(half_neg[:], -0.5).then_inc(consts_pool, 1)
            po.memset(same_hi[:], 1.0).then_inc(consts_pool, 1)
            po.iota(iota_hi[:], [[1, HI], [0, NE]], 0, 0, allow_small_or_imprecise_dtypes=True).then_inc(consts_pool, 1)
            po.iota(iota_lo[:], [[1, LO], [0, NE]], 0, 0, allow_small_or_imprecise_dtypes=True).then_inc(consts_pool, 1)
            po.iota(row1[:], [[0, 1]], 1, 1, allow_small_or_imprecise_dtypes=True).then_inc(consts_pool, 1)
            po.iota(tile_no[:], [[1, T // P]], 0, 0, allow_small_or_imprecise_dtypes=True).then_inc(consts_pool, 1)
            po.wait_ge(consts_pool, 9)
            po.affine_select(out=ident[:], in_=ident[:], compare_op=ALU.not_equal, fill=1.0, base=0,
                             pattern=[[-1, P]], channel_multiplier=1).then_inc(consts_pool, 1)
            po.affine_select(out=upto[:], in_=upto[:], compare_op=ALU.is_ge, fill=0.0, base=0,
                             pattern=[[1, P]], channel_multiplier=-1).then_inc(consts_pool, 1)
            po.affine_select(out=same_hi[:], in_=same_hi[:], compare_op=ALU.is_ge, fill=0.0, base=0,
                             pattern=[[-LO, HI]], channel_multiplier=1).then_inc(consts_pool, 1)
            po.wait_ge(consts_pool, 12)
            po.affine_select(out=same_hi[:], in_=same_hi[:], compare_op=ALU.is_ge, fill=0.0, base=LO - 1,
                             pattern=[[LO, HI]], channel_multiplier=-1).then_inc(consts_pool, 1)

            def rsqrt(n):
                po.wait_ge(veps_done, n)
                po.tensor_tensor(rstd[:], veps[:], half_neg[:], ALU.pow).then_inc(rstd_done, 1)

            def rsqrt2(n):
                po.wait_ge(veps2_done, n)
                po.tensor_tensor(rstd2[:], veps2[:], half_neg[:], ALU.pow).then_inc(rstd2_done, 1)

            def skip(n, u, m):
                po.wait_ge(xn_done, n)
                po.wait_ge(x_in[u], m * 16)
                po.tensor_tensor(xd[:, u], xn[:, u], dskip[:].unsqueeze(1).broadcast_to([P, TT, D]),
                                 ALU.mult).then_inc(dx_done, 1)
                po.wait_ge(dx_done, n)
                po.tensor_tensor(xd[:, u], xd[:, u], xb[:, u], ALU.add).then_inc(xd_done, 1)
                po.wait_ge(xd_done, n)
                po.sem_inc(x_free, 1)

            def scan_input(n):
                if not first(n):
                    po.wait_ge(h_done, (n - 1) * DC)
                for c in range(DC):
                    po.wait_ge(ub_done, (n - 1) * DC + c + 1)
                    po.tensor_tensor(ux[:, c], ub[:, c], xnt[:, c], ALU.mult).then_inc(ux_done, 1)

            def step(n, u, m, early, late):
                if early:
                    rsqrt(n + 1)
                if middle(n):
                    rsqrt2(n)
                if early:
                    skip(n + 1, 1 - u, m)
                    scan_input(n + 1)

            po.wait_ge(consts_in, 16 * 7)
            steps(po, step)

        @block.scalar
        def _(ac):
            ac.preload_act_table_set("natural_log_exp_and_others")
            ac.wait_ge(consts_in, 16 * 7)
            ac.activation(a_exp[:], a_log[:], ACT.Exp).then_inc(aexp_done, 1)
            ac.wait_ge(aexp_done, 1)
            ac.mul(a_neg[:], a_exp[:], -1.0).then_inc(aneg_done, 1)
            ac.wait_ge(aneg_done, 1)

            def softplus(n):
                k = (n - 1) * DC
                ac.preload_act_table_set("natural_log_exp_and_others")
                if not first(n):
                    ac.wait_ge(ux_done, k)
                    ac.wait_ge(h_done, k)
                for c in range(DC):
                    ac.wait_ge(t_done, k + c + 1)
                    ac.copy(xnt[:, c], bank_t[c][:]).then_inc(xnt_done, 1)
                for c in range(DC):
                    ac.wait_ge(d_done, k + c + 1)
                    ac.activation(z[:, c], bank_d[c][:], ACT.Identity, bias=b_dt[:, c:c + 1]).then_inc(z_done, 1)
                for c in range(DC):
                    ac.wait_ge(z_done, k + c + 1)
                    ac.activation(az[:, c], z[:, c], ACT.Abs).then_inc(az_done, 1)
                for c in range(DC):
                    ac.wait_ge(az_done, k + c + 1)
                    ac.activation(ez[:, c], az[:, c], ACT.Exp, scale=-1.0).then_inc(ez_done, 1)
                for c in range(DC):
                    ac.wait_ge(ez_done, k + c + 1)
                    ac.activation(lz[:, c], ez[:, c], ACT.Ln, bias=1.0).then_inc(lz_done, 1)

            def decay(n):
                k = (n - 1) * DC
                for c in range(DC):
                    ac.wait_ge(dt_done, k + c + 1)
                    ac.activation(abar[:, c], dt[:, c], ACT.Exp, scale=a_neg[:, c:c + 1]).then_inc(abar_done, 1)

            def turned2(n):
                for c in range(DC):
                    ac.wait_ge(t2_done, (n - 1) * DC + c + 1)
                    ac.copy(xn2t[:, c], bank_t[c][:]).then_inc(xn2t_done, 1)

            def route(n):
                ac.wait_ge(ls_done, n)
                ac.activation(el[:], ls[:], ACT.Exp).then_inc(el_done, 1)
                ac.wait_ge(wts_done, n)
                ac.wait_ge(x1_done, n * 2)
                ac.dma_start(one(xg_v[ds(n - 1, 1)]), rows[:]).then_inc(rows_out, 16)
                ac.dma_start(one(xa_v[ds(n - 1, 1)]), x1[:]).then_inc(xa_out, 16)

            def step(n, u, m, early, late):
                if early:
                    softplus(n + 1)
                if middle(n):
                    turned2(n)
                if early:
                    decay(n + 1)
                if middle(n):
                    route(n)

            steps(ac, step)
            ac.wait_ge(rows_out, 16 * (NB + 1))
            ac.wait_ge(xa_out, 16 * (NB + 1))

        @block.tensor
        def _(pe):
            pe.wait_ge(consts_in, 16 * 7)
            pe.wait_ge(consts_pool, 13)

            def projections(n, u):
                k = (n - 1) * DC
                pe.wait_ge(xn_done, n)
                for c in range(DC):
                    for t in range(TT):
                        mm = pe.transpose(bank_t[c][:, t * P:(t + 1) * P], xn[:, u, t, c * P:(c + 1) * P], ident[:])
                    mm.then_inc(t_done, 1)
                pe.wait_ge(xnt_done, k + DC)
                if not first(n):
                    pe.wait_ge(z_done, k)
                    pe.wait_ge(ub_done, k)
                    if not (isinstance(n, int) and n == 2):
                        pe.wait_ge(acc_free, n - 2)
                for w, banks, done in ((w_dt, bank_d, d_done), (w_b, bank_b, b_done)):
                    for m in range(DC):
                        for c in range(DC):
                            mm = pe.matmul(banks[m][:], w[:, c, m * P:(m + 1) * P], xnt[:, c],
                                           start=(c == 0), stop=(c == DC - 1))
                        mm.then_inc(done, 1)

            def mixer_out(n, u):
                k = (n - 1) * DC
                pe.wait_ge(h_done, k + DC)
                pe.wait_ge(q_free, n)
                for half in range(2):
                    for t in range(2):
                        tt = half * 2 + t
                        for c in range(DC):
                            mm = pe.matmul(bank_o[half][:, t * D:(t + 1) * D], h[:, u, c, tt * P:(tt + 1) * P],
                                           w_c[:, c], start=(c == 0), stop=(c == DC - 1))
                    mm.then_inc(o_done, 1)

            def router(n):
                k = (n - 1) * DC
                pe.wait_ge(xn2_done, n)
                for c in range(DC):
                    for t in range(TT):
                        mm = pe.transpose(bank_t[c][:, t * P:(t + 1) * P], rows[:, t, c * P:(c + 1) * P], ident[:])
                    mm.then_inc(t2_done, 1)
                pe.wait_ge(xn2t_done, k + DC)
                for t in range(TT):
                    for c in range(DC):
                        mm = pe.matmul(bank_o[0][:, t * NE:(t + 1) * NE], xn2t[:, c, t * P:(t + 1) * P],
                                       w_r[:, c], start=(c == 0), stop=(c == DC - 1))
                mm.then_inc(r_done, 1)

            def positions(n):
                pe.wait_ge(sel_done, n)
                pe.wait_ge(before_done, n)
                opening = True
                for t in range(TT):
                    for lhs, rhs in [(upto, sel[:, t]), (ones, before[:])] + [(ones, sel[:, s]) for s in range(t)]:
                        mm = pe.matmul(bank_o[1][:, t * NE:(t + 1) * NE], lhs[:], rhs, start=opening, stop=False,
                                       skip_group_check=True)
                        opening = False
                mm.then_inc(pos_done, 1)

            def slot_table(n, early):
                pe.wait_ge(hi_done, n * TT)
                pe.wait_ge(v_done, n * TT * 2)
                if early:
                    pe.wait_ge(ub_done, (n + 2) * DC)
                for half in range(2):
                    for gg in range(EG // 2):
                        g = half * (EG // 2) + gg
                        for t in range(TT):
                            mm = pe.matmul(bank_b[half][:, gg * 128:(gg + 1) * 128],
                                           oh_hi[:, t].rearrange("p h e -> p (h e)")[:, g::LO],
                                           oh_v[:, t].rearrange("p v l e -> p (v l e)")[:, g::LO],
                                           start=(gg == 0 and t == 0), stop=(t == TT - 1), skip_group_check=True)
                    mm.then_inc(inv_done, 1)

            def step(n, u, m, early, late):
                if middle(n):
                    mixer_out(n, u)
                if early:
                    projections(n + 1, 1 - u)
                if middle(n):
                    router(n)
                if late:
                    slot_table(n - 1, early)
                if middle(n):
                    positions(n)

            steps(pe, step)
            pe.wait_ge(fin, 2)
            for lo in range(LO):
                mm = pe.matmul(bank_t[0][:, 0:2 * NE], spread[:, lo],
                               slot_m[:, :, :, lo, :].rearrange("p g v e -> p v e g"),
                               start=(lo == 0), stop=(lo == LO - 1))
            mm.then_inc(fin_pe, 1)

        @block.vector
        def _(ve):
            ve.memset(before[:], 0.0).then_inc(zeroed, 1)
            ve.memset(before_f[:], 0.0).then_inc(zeroed, 1)
            ve.memset(slot_acc[:], 0.0).then_inc(zeroed, 1)
            ve.wait_ge(zeroed, 3)
            ve.sem_inc(before_done, 1)
            ve.sem_inc(acc_free, 1)
            ve.sem_inc(q_free, 1)
            ve.sem_inc(rows_out, 16)
            ve.sem_inc(xa_out, 16)
            ve.wait_ge(consts_pool, 13)
            ve.tensor_reduce(same_e[:], ident[:].rearrange("p (h j) -> p j h", j=LO), AX.X, ALU.add).then_inc(same_done, 1)

            def alone(ve):
                ve.nop(nofuse=True)

            def norm(src, st_, mv_, ve_, rs_, dst, n, sems):
                s_stat, s_mv, s_ve, s_rs, s_out = sems
                for t in range(TT):
                    ve.bn_stats(st_[:, t], src(t)).then_inc(s_stat, 1)
                for t in range(TT):
                    ve.wait_ge(s_stat, (n - 1) * TT + t + 1)
                    alone(ve)
                    ve.bn_aggr(mv_[:, t], st_[:, t]).then_inc(s_mv, 1)
                ve.wait_ge(s_mv, n * TT)
                ve.tensor_scalar(ve_[:], mv_[:, :, 1], EPS, None, ALU.add).then_inc(s_ve, 1)
                ve.wait_ge(s_rs, n)
                for t in range(TT):
                    ins = ve.tensor_scalar(dst(t), src(t), mv_[:, t, 0:1], rs_[:, t:t + 1], ALU.subtract, ALU.mult)
                ins.then_inc(s_out, 1)

            def first_norm(n, u, m):
                ve.wait_ge(x_in[u], m * 16)
                norm(lambda t: xb[:, u, t], stat, mv, veps, rstd, lambda t: xn[:, u, t], n,
                     (stat_done, mv_done, veps_done, rstd_done, xn_done))

            def scan_terms(n):
                k = (n - 1) * DC
                for c in range(DC):
                    ve.wait_ge(lz_done, k + c + 1)
                    ve.scalar_tensor_tensor(out=dt[:, c], in0=z[:, c], scalar=0.0, in1=lz[:, c],
                                            op0=ALU.max, op1=ALU.add).then_inc(dt_done, 1)
                for c in range(DC):
                    ve.wait_ge(dt_done, k + c + 1)
                    ve.wait_ge(b_done, k + c + 1)
                    ve.tensor_tensor(ub[:, c], bank_b[c][:], dt[:, c], ALU.mult).then_inc(ub_done, 1)

            def scan(n, u):
                k = (n - 1) * DC
                for c in range(DC):
                    ve.wait_ge(ux_done, k + c + 1)
                    ve.wait_ge(abar_done, k + c + 1)
                    ve.tensor_tensor_scan(h[:, u, c], abar[:, c], ux[:, c], 0.0, ALU.mult, ALU.add).then_inc(h_done, 1)

            def second_norm(n, u):
                ve.wait_ge(rows_out, n * 16)
                ve.wait_ge(xa_out, n * 16)
                for half in range(2):
                    ve.wait_ge(o_done, (n - 1) * 2 + half + 1)
                    ve.wait_ge(xd_done, n)
                    t0 = half * 2
                    ve.tensor_tensor(x1[:, t0:t0 + 2].rearrange("p t d -> p (t d)"), bank_o[half][:],
                                     xd[:, u, t0:t0 + 2].rearrange("p t d -> p (t d)"), ALU.add).then_inc(x1_done, 1)
                ve.wait_ge(x1_done, n * 2)
                norm(lambda t: x1[:, t], stat2, mv2, veps2, rstd2, lambda t: rows[:, t, 0:D], n,
                     (stat2_done, mv2_done, veps2_done, rstd2_done, xn2_done))

            def choose(n):
                ve.wait_ge(r_done, n)
                ve.tensor_copy(lg[:].rearrange("p t e -> p (t e)"), bank_o[0][:, 0:TT * NE]).then_inc(lg_done, 1)
                ve.wait_ge(lg_done, n)
                alone(ve)
                for t in range(TT):
                    ve.max(top8[:, t], lg[:, t]).then_inc(top_done, 1)
                for t in range(TT):
                    ve.wait_ge(top_done, (n - 1) * TT + t + 1)
                    alone(ve)
                    ve.match_replace(lrest[:, t], top8[:, t], lg[:, t], GONE).then_inc(lrest_done, 1)
                ve.tensor_tensor(ls[:], lg[:], top8[:, :, 0:1].broadcast_to([P, TT, NE]), ALU.subtract).then_inc(ls_done, 1)
                ve.wait_ge(lrest_done, n * TT)
                ve.tensor_tensor(sel[:], lg[:], lrest[:], ALU.not_equal).then_inc(sel_done, 1)
                ve.wait_ge(sel_done, n)
                ve.wait_ge(el_done, n)
                ve.tensor_tensor(es[:], el[:], sel[:], ALU.mult).then_inc(es_done, 1)
                ve.wait_ge(es_done, n)
                ve.tensor_reduce(esum[:], es[:], AX.X, ALU.add).then_inc(esum_done, 1)
                ve.wait_ge(esum_done, n)
                ve.reciprocal(erec[:], esum[:]).then_inc(erec_done, 1)
                ve.wait_ge(erec_done, n)
                ve.tensor_tensor(rows[:, :, D:ROW], es[:], erec[:].unsqueeze(2).broadcast_to([P, TT, NE]),
                                 ALU.mult).then_inc(wts_done, 1)
                ve.wait_ge(pos_done, n)
                ve.scalar_tensor_tensor(out=q0[:].rearrange("p t e -> p (t e)"), in0=sel[:].rearrange("p t e -> p (t e)"),
                                        scalar=-1024.0, in1=bank_o[1][:, 0:TT * NE], op0=ALU.mult, op1=ALU.add)\
                    .then_inc(q0_done, 1)
                ve.tensor_reduce(bsum[:], sel[:].rearrange("p t e -> p e t"), AX.X, ALU.add).then_inc(bsum_done, 1)
                ve.wait_ge(q0_done, n)
                ve.sem_inc(q_free, 1)
                ve.tensor_scalar(qi[:], q0[:], 1023.0, None, ALU.add).then_inc(qi_done, 1)
                ve.wait_ge(bsum_done, n)
                ve.tensor_tensor(before_f[:], before_f[:], bsum[:], ALU.add).then_inc(beforef_done, 1)
                ve.wait_ge(qi_done, n)
                ve.tensor_scalar(qh[:], qi[:], 3, None, ALU.arith_shift_right).then_inc(qhl_done, 1)
                ve.tensor_scalar(ql[:], qi[:], LO - 1, None, ALU.bitwise_and).then_inc(qhl_done, 1)
                ve.wait_ge(beforef_done, n)
                ve.tensor_copy(before[:], before_f[:]).then_inc(before_done, 1)
                ve.wait_ge(qhl_done, 2 * n)
                ve.tensor_copy(qhb[:], qh[:]).then_inc(qb_done, 1)
                ve.tensor_copy(qlb[:], ql[:]).then_inc(qb_done, 1)

            def one_hots(n):
                ve.wait_ge(qb_done, 2 * n)
                for t in range(TT):
                    ve.tensor_tensor(oh_hi[:, t], qhb[:, t].unsqueeze(1).broadcast_to([P, HI, NE]), iota_hi[:],
                                     ALU.is_equal).then_inc(hi_done, 1)
                    m = (n - 1) * TT + t
                    ve.tensor_tensor(oh_lo[:], qlb[:, t].unsqueeze(1).broadcast_to([P, LO, NE]), iota_lo[:],
                                     ALU.is_equal).then_inc(lo_done, 1)
                    ve.wait_ge(lo_done, m + 1)
                    ve.tensor_scalar(oh_v[:, t, 0], oh_lo[:], row1[:, 0:1], None, ALU.mult).then_inc(v_done, 1)
                    ve.tensor_scalar(oh_v[:, t, 1], oh_lo[:], tile_no[:, ds(m, 1)], None, ALU.mult).then_inc(v_done, 1)
                    ve.wait_ge(v_done, 2 * m + 2)

            def add_slots(n):
                for half in range(2):
                    ve.wait_ge(inv_done, (n - 1) * 2 + half + 1)
                    part = slot_acc[:, half * (EG // 2):(half + 1) * (EG // 2)].rearrange("p g v l e -> p (g v l e)")
                    ve.tensor_tensor(part, bank_b[half][:], part, ALU.add).then_inc(acc_done, 1)
                ve.wait_ge(acc_done, 2 * n)
                ve.sem_inc(acc_free, 1)

            def step(n, u, m, early, late):
                if early:
                    first_norm(n + 1, 1 - u, m)
                if middle(n):
                    second_norm(n, u)
                if late:
                    one_hots(n - 1)
                if early:
                    scan_terms(n + 1)
                if middle(n):
                    choose(n)
                if early:
                    scan(n + 1, 1 - u)
                if late:
                    add_slots(n - 1)

            steps(ve, step)
            ve.wait_ge(same_done, 1)
            ve.tensor_tensor(slot_m[:].rearrange("p g v l e -> p (g v l) e"),
                             slot_acc[:].rearrange("p g v l e -> p (g v l) e"),
                             same_e[:].unsqueeze(1).broadcast_to([P, EG * 2 * LO, LO]), ALU.mult).then_inc(fin, 1)
            ve.memset(spread[:], 0.0).then_inc(zeroed, 1)
            ve.wait_ge(zeroed, 4)
            for lo in range(LO):
                ins = ve.tensor_copy(spread[:, lo, :, lo], same_hi[:])
            ins.then_inc(fin, 1)
            ve.wait_ge(fin_pe, 1)
            ve.tensor_copy(tokf[:].rearrange("p v e -> p (v e)"), bank_t[0][:, 0:2 * NE]).then_inc(fin, 1)
            ve.wait_ge(fin, 3)
            ve.scalar_tensor_tensor(out=tid[:], in0=tokf[:, 1], scalar=float(P), in1=tokf[:, 0],
                                    op0=ALU.mult, op1=ALU.add).then_inc(fin, 1)
            ve.tensor_scalar(emp[:], tokf[:, 0], 0.5, float(2 * T), ALU.is_lt, ALU.mult).then_inc(fin, 1)
            ve.wait_ge(fin, 5)
            ve.tensor_scalar(gf[:], tid[:], -1.0, 0.0, ALU.add, ALU.max).then_inc(fin, 1)
            ve.scalar_tensor_tensor(out=sf[:], in0=tid[:], scalar=-1.0, in1=emp[:], op0=ALU.add, op1=ALU.add)\
                .then_inc(fin, 1)
            ve.wait_ge(fin, 7)
            ve.tensor_copy(slots[:, :, 0], gf[:]).then_inc(fin, 1)
            ve.tensor_copy(slots[:, :, 1], sf[:]).then_inc(fin, 1)
            ve.wait_ge(fin, 9)

        block.__exit__(None, None, None)
        sp.clear()


def stage2(nc, a, acc, xg, slots, codes, scales, wffn, w):
    R = 8
    PIECE = 3 * FN // NE
    with ExitStack() as st:
        sp = Space(nc, st, "s2_")
        sb, sem = sp.sb, sp.sem
        ident = sb("ident2", [P, P])
        w_gu = sb("w_gu", [P, R, DC, 2 * FF])
        w_dn = sb("w_dn", [P, R, D])
        gidx = sb("gidx", [P, R, 1], I32)
        sidx = sb("sidx", [P, R, 1], I32)
        xe = sb("xe", [P, R, ROW])
        xet = sb("xet", [P, 2, DC, P])
        sg = sb("sg", [P, 2, P])
        hh = sb("hh", [P, 2, P])
        ys = sb("ys", [P, R, D])
        bv_sb = sb("bv_sb", [P, NKV])
        bvb = sb("bvb", [P, NKV, P])
        bo_sb = sb("bo_sb", [P, D])
        wvt_sb = sb("wvt_sb", [P, NKV, LAT])
        wo_sb = sb("wo_sb", [P, NH, D])
        mag = sb("mag", [P, 2, PIECE], I32)
        sgn = sb("sgn", [P, 2, PIECE], I32)
        va = sb("va", [P, 2, PIECE])
        vb = sb("vb", [P, 2, PIECE])
        vc = sb("vc", [P, 2, PIECE])
        vd = sb("vd", [P, 2, PIECE])
        vs = sb("vs", [P, 2, 2, PIECE])
        bank_t = sp.banks("bank2_t", 2)
        bank_g = sp.banks("bank2_g", 2)
        bank_y = sp.banks("bank2_y", 2)
        bank_v = sp.banks("bank2_v", 1)[0]
        bank_o = sp.banks("bank2_o", 1)[0]

        id0 = sem("id0")
        id_done = sem("id_done")
        w_in = [sem(f"w_in{j}") for j in range(R)]
        w3_in = sem("w3_in")
        bvb_done = sem("bvb_done")
        wvt_done = sem("wvt_done")
        wvo_done = sem("wvo_done")
        ob_done = sem("ob_done")
        obias_done = sem("obias_done")
        gidx_done = sem("gidx_done")
        sidx_done = sem("sidx_done")
        vs_done = sem("vs_done")
        xe_in = [sem(f"xe_in{j}") for j in range(R)]
        t_done = sem("te_done")
        xet_done = sem("xet_done")
        gu_done = sem("gu_done")
        sg_done = sem("sg_done")
        hh_done = sem("hh_done")
        y_done = sem("y_done")
        ys_done = sem("ys_done")
        added = [sem(f"added{j}") for j in range(NCH)]
        mag_done = sem("mag_done")
        va_done = sem("va_done")
        vb_done = sem("vb_done")
        vc_done = sem("vc_done")
        vd_done = sem("vd_done")
        wffn_done = sem("wffn_done")

        gu_v = a["L0_ffn_gate_up_proj"].rearrange("e (c p) f -> e p c f", p=P)
        dn_v = a["L0_ffn_down_proj"]
        loads = ((w["wq"][:], a["wq"].rearrange("(c p) n -> p c n", p=P)),
                 (w["wqsel"][:], a["wqsel"].rearrange("(c p) n -> p c n", p=P)),
                 (w["wkd"][:], a["L1_attn_Wkd"].rearrange("(c p) n -> p c n", p=P)),
                 (w["wkk"][0:LAT], a["wkk"].rearrange("l (g n) -> l g n", g=NKV)),
                 (w["wksel"][0:LAT], a["wksel"]),
                 (w["bq"][:], a["bq"]), (w["bk"][:], a["bk"]), (w["bkd"][0:LAT], a["bkd"]),
                 (w["bqsel"][0:SELD], a["bqsel"]), (w["bksel"][0:SELD], a["bksel"]),
                 (w["rcos"][:], a["rcos"]), (w["rsin"][:], a["rsin"]),
                 (wo_sb[:], a["L1_attn_Wo"].rearrange("(h p) d -> p h d", p=P)),
                 (wvt_sb[:], a["wvt"]),
                 (bo_sb[:], a["L1_attn_bo"].partition_broadcast(P)), (bv_sb[:], a["bv"]))

        block = nc.Block()
        block.__enter__()

        def known(e):
            return isinstance(e, int)

        def pair(e):
            return e - (NE - NH // 2) if known(e) and e >= NE - NH // 2 else None

        def adds(i, j):
            return i * (R // NCH) + j // NCH

        def past(eng, sem_, value):
            if not known(value) or value > 0:
                eng.wait_ge(sem_, value)

        def steps(eng, step):
            for j in range(R):
                step(j, j, 0)
            with eng.Fori(1, NE // R - 1) as i:
                for j in range(R):
                    step(i * R + j, j, i)
            for j in range(R):
                step(NE - R + j, j, NE // R - 1)

        @block.sync
        def _(sy):
            def load(e, j):
                sy.dma_start(w_gu[:, j], gu_v[ds(e, 1)].rearrange("o p c f -> (o p) c f")).then_inc(w_in[j], 16)
                sy.dma_start(w_dn[0:FF, j], dn_v[ds(e, 1)].rearrange("o f d -> (o f) d")).then_inc(w_in[j], 16)

            for j in range(R):
                load(j, j)
            for dst, src in loads:
                sy.dma_start(dst, src).then_inc(w3_in, 16)
            with sy.Fori(0, NE // R - 1) as i:
                for j in range(R):
                    sy.wait_ge(y_done, i * R + j + 1)
                    load(i * R + j + R, j)
            sy.wait_ge(w3_in, 16 * len(loads))

        @block.gpsimd
        def _(po):
            po.memset(ident[:], 0.0).then_inc(id0, 1)
            po.wait_ge(id0, 1)
            po.affine_select(out=ident[:], in_=ident[:], compare_op=ALU.not_equal, fill=1.0, base=0,
                             pattern=[[-1, P]], channel_multiplier=1).then_inc(id_done, 1)

            def gather(e, j):
                po.wait_ge(gidx_done, e + 1)
                po.nop(nofuse=True)
                po.indirect_dma_start(xe[:, j], None, xg, bass.IndirectOffsetOnAxis(ap=gidx[:, j], axis=0))\
                    .then_inc(xe_in[j], 16)

            def scatter(e, j, i):
                po.wait_ge(ys_done, e + 1)
                po.wait_ge(sidx_done, e + 1)
                c = j % NCH
                past(po, added[c], adds(i, j) * 16)
                po.nop(nofuse=True)
                po.indirect_dma_start(acc[c], bass.IndirectOffsetOnAxis(ap=sidx[:, j], axis=0), ys[:, j], None,
                                      bounds_check=T - 1, oob_is_err=False, compute_op=ALU.add)\
                    .then_inc(added[c], 16)

            for j in range(R - 1):
                gather(j, j)

            def step(e, j, i):
                if not known(e) or e + R - 1 < NE:
                    gather(e + R - 1, (j + R - 1) % R)
                scatter(e, j, i)
                po.wait_ge(vs_done, e + 1)
                po.tensor_tensor(wffn[:, :, ds(e * PIECE, PIECE)], vs[:, j % 2],
                                 scales[:, ds(e * PIECE, PIECE)].unsqueeze(1).broadcast_to([P, 2, PIECE]),
                                 ALU.mult).then_inc(wffn_done, 1)

            steps(po, step)
            for c in range(NCH):
                po.wait_ge(added[c], 16 * (NE // NCH))

        @block.scalar
        def _(ac):
            def turned(e, j):
                ac.wait_ge(t_done, e + 1)
                ac.copy(xet[:, j % 2].rearrange("p c s -> p (c s)"), bank_t[j % 2][:, 0:DC * P]).then_inc(xet_done, 1)

            def gate(e, j):
                ac.wait_ge(gu_done, e + 1)
                ac.activation(sg[0:FF, j % 2], bank_g[j % 2][0:FF, 0:P], ACT.Silu).then_inc(sg_done, 1)

            def weigh(e, j):
                ac.wait_ge(y_done, e + 1)
                ac.activation(ys[:, j], bank_y[j % 2][:, 0:D], ACT.Copy, scale=xe[:, j, ds(e + D, 1)])\
                    .then_inc(ys_done, 1)

            def value_output(hp):
                ac.wait_ge(wvt_done, hp + 1)
                ac.copy(w["wvo"][0:LAT, hp], bank_v[0:LAT, 0:D])
                ac.copy(w["wvo"][LAT:P, hp], bank_v[0:LAT, D:2 * D]).then_inc(wvo_done, 1)

            def step(e, j, i):
                if pair(e) is not None:
                    value_output(pair(e))
                if not known(e) or e + 2 < NE:
                    turned(e + 2, j + 2)
                if not known(e) or e + 1 < NE:
                    gate(e + 1, j + 1)
                past(ac, added[j % NCH], (adds(i, j) - R // NCH + 1) * 16)
                weigh(e, j)

            turned(0, 0)
            turned(1, 1)
            gate(0, 0)
            steps(ac, step)

        @block.tensor
        def _(pe):
            pe.wait_ge(id_done, 1)

            def turn(e, j, i):
                pe.wait_ge(xe_in[j % R], i * 16 + 16)
                for c in range(DC):
                    mm = pe.transpose(bank_t[j % 2][:, c * P:(c + 1) * P], xe[:, j % R, c * P:(c + 1) * P], ident[:])
                mm.then_inc(t_done, 1)

            def gate_up(e, j, i):
                pe.wait_ge(xet_done, e + 1)
                pe.wait_ge(w_in[j % R], i * 32 + 32)
                for part in range(2):
                    for c in range(DC):
                        mm = pe.matmul(bank_g[j % 2][0:FF, part * P:(part + 1) * P],
                                       w_gu[:, j % R, c, part * FF:(part + 1) * FF], xet[:, j % 2, c],
                                       start=(c == 0), stop=(c == DC - 1))
                mm.then_inc(gu_done, 1)

            def down(e, j):
                pe.wait_ge(hh_done, e + 1)
                pe.matmul(bank_y[j % 2][:, 0:D], hh[0:FF, j % 2], w_dn[0:FF, j], start=True, stop=True)\
                    .then_inc(y_done, 1)

            def value_output(hp):
                pe.wait_ge(w3_in, 16 * len(loads))
                if hp > 0:
                    pe.wait_ge(wvo_done, hp)
                for i in range(2):
                    h = hp * 2 + i
                    mm = pe.matmul(bank_v[0:LAT, i * D:(i + 1) * D], wvt_sb[:, h // G], wo_sb[:, h],
                                   start=(i == 0), stop=True, skip_group_check=True)
                mm.then_inc(wvt_done, 1)
                pe.wait_ge(bvb_done, NKV)
                for i in range(2):
                    h = hp * 2 + i
                    mm = pe.matmul(bank_o[:, 0:D], bvb[:, h // G], wo_sb[:, h], start=(h == 0), stop=(h == NH - 1))
                mm.then_inc(ob_done, 1)

            def step(e, j, i):
                if pair(e) is not None:
                    value_output(pair(e))
                if not known(e) or e + 2 < NE:
                    turn(e + 2, j + 2, i + (j + 2) // R)
                if not known(e) or e + 1 < NE:
                    gate_up(e + 1, j + 1, i + (j + 1) // R)
                down(e, j)

            turn(0, 0, 0)
            turn(1, 1, 0)
            gate_up(0, 0, 0)
            steps(pe, step)

        @block.vector
        def _(ve):
            def gather_index(e, j):
                ve.tensor_copy(gidx[:, j], slots[:, ds(e, 1), 0]).then_inc(gidx_done, 1)

            def scatter_index(e, j):
                ve.tensor_copy(sidx[:, j], slots[:, ds(e, 1), 1]).then_inc(sidx_done, 1)

            def hidden(e, j):
                ve.wait_ge(sg_done, e + 1)
                ve.tensor_tensor(hh[0:FF, j % 2], bank_g[j % 2][0:FF, P:2 * P], sg[0:FF, j % 2], ALU.mult)\
                    .then_inc(hh_done, 1)

            def dequantise(e, j):
                w = codes[:, ds(e * PIECE, PIECE)]
                ve.tensor_scalar(mag[:, 0], w, 7, None, ALU.bitwise_and).then_inc(mag_done, 1)
                ve.tensor_scalar(mag[:, 1], w, 4, 7, ALU.arith_shift_right, ALU.bitwise_and).then_inc(mag_done, 1)
                ve.tensor_scalar(sgn[:, 0], w, 8, None, ALU.bitwise_and).then_inc(mag_done, 1)
                ve.tensor_scalar(sgn[:, 1], w, 4, 8, ALU.arith_shift_right, ALU.bitwise_and).then_inc(mag_done, 1)
                ve.wait_ge(mag_done, e * 4 + 4)
                ve.tensor_scalar(va[:], mag[:], 2.0, -8.0, ALU.mult, ALU.add).then_inc(va_done, 1)
                ve.tensor_scalar(vd[:], sgn[:], -0.25, 1.0, ALU.mult, ALU.add).then_inc(vd_done, 1)
                ve.wait_ge(va_done, e + 1)
                ve.scalar_tensor_tensor(out=vb[:], in0=mag[:], scalar=-2.0, in1=va[:], op0=ALU.add, op1=ALU.max)\
                    .then_inc(vb_done, 1)
                ve.wait_ge(vb_done, e + 1)
                ve.scalar_tensor_tensor(out=vc[:], in0=mag[:], scalar=0.5, in1=vb[:], op0=ALU.mult, op1=ALU.max)\
                    .then_inc(vc_done, 1)
                ve.wait_ge(vc_done, e + 1)
                ve.wait_ge(vd_done, e + 1)
                past(ve, wffn_done, e - 1)
                ve.tensor_tensor(vs[:, j % 2], vc[:], vd[:], ALU.mult).then_inc(vs_done, 1)

            def step(e, j, i):
                if pair(e) == 0:
                    ve.wait_ge(w3_in, 16 * len(loads))
                    for g in range(NKV):
                        ve.tensor_copy(bvb[:, g], bv_sb[:, g:g + 1].broadcast_to([P, P])).then_inc(bvb_done, 1)
                if not known(e) or e + 1 < NE:
                    hidden(e + 1, j + 1)
                if not known(e) or e + R - 1 < NE:
                    gather_index(e + R - 1, (j + R - 1) % R)
                past(ve, added[j % NCH], (adds(i, j) - R // NCH + 1) * 16)
                scatter_index(e, j)
                dequantise(e, j)

            for j in range(R - 1):
                gather_index(j, j)
            hidden(0, 0)
            steps(ve, step)
            ve.wait_ge(ob_done, NH // 2)
            ve.tensor_tensor(w["obias"][:], bank_o[:, 0:D], bo_sb[:], ALU.add).then_inc(obias_done, 1)
            ve.wait_ge(wffn_done, NE)
            ve.wait_ge(obias_done, 1)

        block.__exit__(None, None, None)
        sp.clear()


def stage3(nc, acc, wffn, w, work, out):
    H2 = HD // 2
    QS = float(HD) ** -0.5
    AUG = LAT + 1
    WIDE = S + (TT - 1) * P
    with ExitStack() as st:
        sp = Space(nc, st, "s3_")
        sb, sem = sp.sb, sp.sem
        ident = sb("ident3", [P, P])
        half_neg = sb("half_neg3", [P, TT])
        zero_w = sb("zero_w", [P, P], BF16)
        wqs = sb("wqs", [P, 4, DC, HD])
        w_hi = sb("w_hi", [P, 2, 2, 2, P], F32R)
        w_lo = sb("w_lo", [P, 2, 2, 2, P], F32R)
        causal = sb("causal", [P, WIDE])
        offdiag = sb("offdiag", [P, WIDE])
        bnbuf = sb("bnbuf", [P, TT, 6])
        bnbuf4 = sb("bnbuf4", [P, TT, 6])
        mv3 = sb("mv3", [P, TT, 2])
        mv4 = sb("mv4", [P, TT, 2])
        veps3 = sb("veps3", [P, TT])
        veps4 = sb("veps4", [P, TT])
        rstd3 = sb("rstd3", [P, TT])
        rstd4 = sb("rstd4", [P, TT])
        xin = [sb(f"xin{c}", [P, TT, D]) for c in range(NCH)]
        xn3 = sb("xn3", [P, TT, D])
        xo = sb("xo", [P, TT, D])
        x4 = sb("x4", [P, TT, D])
        xn4 = sb("xn4", [P, TT, D])
        xn3t = sb("xn3t", [P, DC, S])
        xn4_hi = sb("xn4_hi", [P, 2, S], F32R)
        xn4_lo = sb("xn4_lo", [P, 2, S], F32R)
        kvdt = sb("kvdt", [P, S])
        kva = sb("kva", [P, TT, AUG])
        qsel = sb("qsel", [P, S])
        ksel = sb("ksel", [P, S])
        qst = sb("qst", [P, P])
        qa = sb("qa", [P, S])
        qb = sb("qb", [P, S])
        qr = sb("qr", [P, 4, S])
        s0 = sb("s0", [P, S])
        m8 = sb("m8", [P, 8])
        nm = sb("nm", [P, 2, 1])
        rec = sb("rec", [P, TT])
        def carve(*shapes):
            at = 0
            for names, shape in shapes:
                size = int(np.prod(shape))
                yield work[:, at:at + size].rearrange(f"p ({names}) -> p {names}", **dict(zip(names.split(), shape)))
                at += size

        ym, mask, pr, kr, sm, pt = carve(("t h l", (TT, NH, LAT)), ("t n", (TT, S)), ("t n", (TT, S)),
                                         ("g n", (NKV, S)), ("s n", (2, S)), ("s n", (2, S)))
        wq, wqsel, wkd, wkk, wksel, wvo = (w[n] for n in ("wq", "wqsel", "wkd", "wkk", "wksel", "wvo"))
        bq, bk, bkd, bqsel, bksel = (w[n] for n in ("bq", "bk", "bkd", "bqsel", "bksel"))
        obias, rcos, rsin = (w[n] for n in ("obias", "rcos", "rsin"))
        gl, it = pr[:, 0:2], pr[:, 2:4]
        yt = qr[:].rearrange("p j n -> p (j n)").rearrange("p (s c q) -> p s c q", s=2, c=NH // 2)
        sr = sm
        eq, eo = pt[:, 0], pt[:, 1]
        ka, kb = qa, qb
        xs, ob = xin[0], xn4

        bq_ = sp.banks("bank3_q", 2)
        bs = sp.banks("bank3_s", 2)
        bp = sp.banks("bank3_p", 2)
        by = sp.banks("bank3_y", 2)

        names = """c0 c3 xs_done stat3 agg3 ve3 rs3 xn3_done xo_done
            t3_done xn3t_done kvd_done kvdt_done kvt_done kva_done qk_done qksel_done k_done krope_a krope_done kr_done
            q_done qrope_a qrope_done qr_done s_done ttr_done exp_done tp_done pte_done pv_done rec_done norm_done
            yt_done yte_done o_done x4_done stat4 agg4 ve4 rs4 xn4_done t4_done xn4hi_done xn4lo_done whi_done wlo_done
            qst_done ms_done s0_done mx_done mr_done eq_done eo_done mask_done
            g_done u_done gelu_done inter_done dn_done fo_done out_done""".split()
        sems = {n: sem(n) for n in names}
        (c0, c3, xs_done, stat3, agg3, ve3, rs3, xn3_done, xo_done,
         t3_done, xn3t_done, kvd_done, kvdt_done, kvt_done, kva_done, qk_done, qksel_done, k_done, krope_a,
         krope_done, kr_done, q_done, qrope_a, qrope_done, qr_done, s_done, ttr_done, exp_done, tp_done, pte_done,
         pv_done, rec_done, norm_done, yt_done, yte_done, o_done, x4_done, stat4, agg4, ve4, rs4, xn4_done,
         t4_done, xn4hi_done, xn4lo_done, whi_done, wlo_done, qst_done, ms_done, s0_done, mx_done, mr_done, eq_done, eo_done, mask_done,
         g_done, u_done, gelu_done, inter_done, dn_done, fo_done, out_done) = (sems[n] for n in names)
        x_in = [sem(f"x3_in{c}") for c in range(NCH)]
        wq_in = [sem(f"wq_in{j}") for j in range(4)]

        acc_v = [x.rearrange("(b t p) d -> b p t d", t=TT, p=P) for x in acc]
        out_v = out.rearrange("b (t p) d -> b p t d", p=P)
        PARTS4 = ((0, 0, TT - 1), (1, TT - 1, TT))

        def one(ap):
            return ap.rearrange("o p t d -> (o p) t d")

        def quads(eng, step):
            with eng.Fori(0, 3) as g:
                for j in range(4):
                    step(g, j)
            for j in range(4):
                step(3, j)

        def ffn_weights(g, j):
            return wffn[:, :, 0:2 * FN].rearrange("p c (w n) -> p c w n", w=2)[:, :, :, ds((g * 4 + j) * P, P)]

        def two_on(g, j):
            return None if isinstance(g, int) and g * 4 + j + 2 > 15 else (g + (j + 2) // 4, (j + 2) % 4)

        def alone(eng):
            eng.nop(nofuse=True)

        def query_bank(g, j):
            return bs[j] if isinstance(g, int) and g == 0 and j < 2 else bq_[j % 2]

        def at(g, j, *place):
            return isinstance(g, int) and (g, j) == place

        def final(g, j):
            return at(g, j, 3, 3)

        def following(g, j):
            return None if final(g, j) else (g + (j + 1) // 4, (j + 1) % 4)

        def tiles():
            return [(o, TT - 1 - o) for o in range(TT)]

        block = nc.Block()
        block.__enter__()

        @block.sync
        def _(sy):
            def load_x(b):
                if not isinstance(b, int):
                    sy.wait_ge(xo_done, b)
                    sy.wait_ge(xn3_done, b)
                for c in range(NCH):
                    sy.dma_start(xin[c][:], one(acc_v[c][ds(b, 1)])).then_inc(x_in[c], 16)

            def stage_q(g, j):
                sy.dma_start(wqs[:, j], wq[:, :, ds((g * 4 + j) * HD, HD)]).then_inc(wq_in[j], 16)

            load_x(0)
            for j in range(4):
                stage_q(0, j)

            def sequence(b, more):
                if more:
                    load_x(b + 1)
                with sy.Fori(0, 3) as g:
                    for j in range(4):
                        sy.wait_ge(q_done, b * 16 + g * 4 + j + 1)
                        stage_q(g + 1, j)
                if more:
                    for j in range(4):
                        sy.wait_ge(q_done, b * 16 + 12 + j + 1)
                        stage_q(0, j)
                sy.wait_ge(fo_done, b * 2 + 2 + 2)
                sy.dma_start(one(out_v[ds(b, 1)]), ob[:]).then_inc(out_done, 16)

            with sy.Fori(0, NB - 1) as b:
                sequence(b, True)
            sequence(NB - 1, False)
            sy.wait_ge(out_done, 16 * (NB + 1))

        @block.gpsimd
        def _(po):
            po.memset(ident[:], 0.0).then_inc(c0, 1)
            po.memset(causal[:], 0.0).then_inc(c0, 1)
            po.memset(offdiag[:], NEG).then_inc(c0, 1)
            po.memset(half_neg[:], -0.5).then_inc(c0, 1)
            po.memset(zero_w[:], 0.0).then_inc(c0, 1)
            po.memset(kva[:], 1.0).then_inc(c0, 1)
            po.wait_ge(c0, 6)
            po.affine_select(out=ident[:], in_=ident[:], compare_op=ALU.not_equal, fill=1.0, base=0,
                             pattern=[[-1, P]], channel_multiplier=1).then_inc(c3, 1)
            po.affine_select(out=causal[:], in_=causal[:], compare_op=ALU.is_ge, fill=NEG, base=(TT - 1) * P,
                             pattern=[[-1, WIDE]], channel_multiplier=1).then_inc(c3, 1)
            po.affine_select(out=offdiag[:], in_=offdiag[:], compare_op=ALU.not_equal, fill=0.0,
                             base=(TT - 1) * P, pattern=[[-1, WIDE]], channel_multiplier=1).then_inc(c3, 1)
            po.sem_inc(qr_done, 1)
            po.sem_inc(kr_done, 1)

            def sum_chains(b, half):
                if half == 0:
                    for c in range(NCH):
                        po.wait_ge(x_in[c], b * 16 + 16)
                t0 = half * 2
                po.tensor_tensor(xs[:, t0:t0 + 2], xin[0][:, t0:t0 + 2], xin[1][:, t0:t0 + 2], ALU.add)\
                    .then_inc(xs_done, 1)

            def first_norm(b):
                po.wait_ge(ve3, b + 1)
                po.tensor_tensor(rstd3[:], veps3[:], half_neg[:], ALU.pow).then_inc(rs3, 1)

            def keys(b, g):
                po.wait_ge(krope_done, b * 4 + g + 1 + 2)
                po.tensor_tensor(kr[:, g], ka[:], kb[:], ALU.add).then_inc(kr_done, 1)

            def residual(b):
                po.wait_ge(x4_done, b * 4 + 2)
                po.wait_ge(xs_done, b * 2 + 2)
                po.tensor_tensor(xo[:], xs[:], obias[:].unsqueeze(1).broadcast_to([P, TT, D]), ALU.add)\
                    .then_inc(xo_done, 1)

            def rotate(b, g, j):
                c = g * 4 + j
                po.wait_ge(qrope_done, b * 16 + c + 1 + 2)
                po.tensor_tensor(qr[:, j], qa[:], qb[:], ALU.add).then_inc(qr_done, 1)

            def attention(b, more):
                for half in range(2):
                    rotate(b, 0, 2 + half)
                    if more:
                        sum_chains(b + 1, half)
                with po.Fori(1, 3) as g:
                    for j in range(4):
                        rotate(b, g, j)
                for j in range(4):
                    rotate(b, 3, j)
                    if more and j == 2:
                        first_norm(b + 1)

            def low_weights(b, g, j):
                po.wait_ge(whi_done, b * 16 + g * 4 + j + 1)
                po.tensor_tensor(w_lo[:, j % 2], ffn_weights(g, j), w_hi[:, j % 2].bitcast(F32), ALU.subtract)\
                    .then_inc(wlo_done, 1)

            def feed_forward(b):
                low_weights(b, 0, 2)
                low_weights(b, 0, 3)
                with po.Fori(1, 4) as g:
                    for j in range(4):
                        low_weights(b, g, j)

            def starts(b):
                rotate(b, 0, 0)
                rotate(b, 0, 1)

            def second_norm(b):
                for part, lo, hi in PARTS4:
                    po.wait_ge(ve4, b * 2 + part + 1)
                    po.tensor_tensor(rstd4[:, lo:hi], veps4[:, lo:hi], half_neg[:, lo:hi], ALU.pow).then_inc(rs4, 1)

            sum_chains(0, 0)
            sum_chains(0, 1)
            first_norm(0)
            for g in range(NKV):
                keys(0, g)
            residual(0)
            starts(0)
            low_weights(0, 0, 0)
            low_weights(0, 0, 1)
            with po.Fori(0, NB - 1) as b:
                attention(b, True)
                for g in range(NKV):
                    keys(b + 1, g)
                second_norm(b)
                residual(b + 1)
                starts(b + 1)
                feed_forward(b)
                low_weights(b + 1, 0, 0)
                low_weights(b + 1, 0, 1)
            attention(NB - 1, False)
            second_norm(NB - 1)
            feed_forward(NB - 1)

        @block.scalar
        def _(ac):
            ac.sem_inc(exp_done, 2)
            ac.sem_inc(pte_done, 2)
            ac.sem_inc(yte_done, 2)
            ac.sem_inc(gelu_done, 2)

            def front(b):
                for c in range(DC):
                    ac.wait_ge(t3_done, b * 2 + c + 1)
                    ac.copy(xn3t[:, c], bq_[c][:]).then_inc(xn3t_done, 1)

            def latents(b):
                ac.wait_ge(kvd_done, b + 1)
                ac.activation(kvdt[0:LAT], bq_[0][0:LAT, :], ACT.Identity, bias=bkd[0:LAT]).then_inc(kvdt_done, 1)

            def selectors(b):
                ac.wait_ge(qk_done, b + 1)
                ac.activation(qsel[0:SELD], bq_[1][0:SELD, :], ACT.Identity, bias=bqsel[0:SELD]).then_inc(qksel_done, 1)
                ac.activation(ksel[0:SELD], bq_[0][0:SELD, :], ACT.Identity, bias=bksel[0:SELD]).then_inc(qksel_done, 1)

            def latent_rows(b):
                ac.wait_ge(kvt_done, b + 1)
                ac.copy(kva[:, :, 0:LAT], by[1][:, 0:TT * LAT].rearrange("p (t l) -> p t l", l=LAT)).then_inc(kva_done, 1)

            def select_query(b, o):
                ac.wait_ge(ms_done, b * 4 + o + 1)
                ac.wait_ge(qksel_done, b * 2 + 2)
                ac.copy(qst[0:SELD], qsel[0:SELD, ds((TT - 1) * P - o * P, P)]).then_inc(qst_done, 1)

            def exponents(b, g, j, o):
                t = TT - 1 - o
                n = (t + 1) * P
                ac.wait_ge(ttr_done, (b * 16 + g * 4 + j) * 4 + o + 1 + 2)
                ac.activation(pr[:, t, 0:n], sm[:, o % 2, 0:n], ACT.Exp, bias=nm[:, o % 2], scale=-1.0)\
                    .then_inc(exp_done, 1)

            def head(b, g, j, more):
                k = (b * 16 + g * 4 + j) * 4
                if final(g, j) and more:
                    selectors(b + 1)
                for o, t in tiles():
                    n = (t + 1) * P
                    ac.wait_ge(tp_done, k + o + 1)
                    ac.wait_ge(pv_done, k + o + 1)
                    ac.copy(pt[:, o % 2, 0:n], bp[o % 2][:, 0:n]).then_inc(pte_done, 1)
                    if o == 0 and at(g, j, 3, 2) and more:
                        front(b + 1)
                    if o > 0 and following(g, j):
                        exponents(b, *following(g, j), o - 1)
                    if o == 1 and at(g, j, 3, 2) and more:
                        latents(b + 1)
                if following(g, j):
                    exponents(b, *following(g, j), TT - 1)

            def turned(b, t):
                for half in range(2):
                    ac.wait_ge(yt_done, b * 8 + t * 2 + half + 1)
                    ac.wait_ge(o_done, b * 4 + t + 1)
                    ac.copy(yt[:, t % 2, half * 4:half * 4 + 4].rearrange("p c q -> p (c q)"), bp[half][:])\
                        .then_inc(yte_done, 1)

            def turned4(b):
                for c in range(2):
                    ac.wait_ge(t4_done, b * 2 + c + 1)
                    ac.copy(xn4_hi[:, c], bp[c][:]).then_inc(xn4hi_done, 1)

            def high_weights(b, g, j):
                ac.copy(w_hi[:, j % 2], ffn_weights(g, j)).then_inc(whi_done, 1)

            def gelu(b, g, j):
                f = b * 16 + g * 4 + j
                ac.wait_ge(g_done, f + 1)
                ac.wait_ge(inter_done, f + 1)
                ac.activation(gl[:, j % 2], bq_[j % 2][:], ACT.Gelu_apprx_tanh).then_inc(gelu_done, 1)

            front(0)
            latents(0)
            selectors(0)
            select_query(0, 0)
            latent_rows(0)
            with ac.Fori(1, TT) as i:
                select_query(0, i)
            high_weights(0, 0, 0)
            high_weights(0, 0, 1)

            def sequence(b, more):
                for o in range(TT):
                    exponents(b, 0, 0, o)
                quads(ac, lambda g, j: head(b, g, j, more))
                turned(b, 0)
                turned(b, 1)
                if more:
                    latent_rows(b + 1)
                turned(b, 2)
                turned(b, 3)
                if more:
                    select_query(b + 1, 0)
                turned4(b)

                def chunk(g, j):
                    gelu(b, g, j)
                    if two_on(g, j):
                        ac.wait_ge(u_done, b * 16 + g * 4 + j + 1)
                        high_weights(b, *two_on(g, j))
                    if j == 2 and more and not (isinstance(g, int) and g == 3):
                        select_query(b + 1, g + 1)

                quads(ac, chunk)
                if more:
                    for j in range(2):
                        ac.wait_ge(u_done, b * 16 + 15 + j)
                        high_weights(b + 1, 0, j)

            with ac.Fori(0, NB - 1) as b:
                sequence(b, True)
            sequence(NB - 1, False)

        @block.tensor
        def _(pe):
            pe.sem_inc(pv_done, 2)
            pe.sem_inc(o_done, 2)
            pe.sem_inc(ms_done, 1)
            pe.sem_inc(dn_done, 2)
            pe.wait_ge(c3, 3)

            def front(b):
                pe.wait_ge(xn3_done, b + 1)
                for c in range(DC):
                    for t in range(TT):
                        mm = pe.transpose(bq_[c][:, t * P:(t + 1) * P], xn3[:, t, c * P:(c + 1) * P], ident[:])
                    mm.then_inc(t3_done, 1)

            def latents(b):
                pe.wait_ge(xn3t_done, b * 2 + 2)
                alone(pe)
                for c in range(DC):
                    mm = pe.matmul(bq_[0][0:LAT, :], wkd[:, c], xn3t[:, c], start=(c == 0), stop=(c == DC - 1))
                mm.then_inc(kvd_done, 1)

            def selectors(b):
                for c in range(DC):
                    pe.matmul(bq_[1][0:SELD, :], wqsel[:, c], xn3t[:, c], start=(c == 0), stop=(c == DC - 1))
                pe.wait_ge(kvdt_done, b + 1)
                alone(pe)
                pe.matmul(bq_[0][0:SELD, :], wksel[0:LAT], kvdt[0:LAT], start=True, stop=True).then_inc(qk_done, 1)

            def latent_rows(b):
                for t in range(TT):
                    mm = pe.transpose(by[1][:, t * LAT:(t + 1) * LAT], kvdt[0:LAT, t * P:(t + 1) * P], ident[0:LAT, 0:LAT])
                mm.then_inc(kvt_done, 1)

            def keys(b, g):
                pe.wait_ge(qksel_done, b * 2 + 2)
                pe.wait_ge(krope_done, b * 4 + g + 1)
                alone(pe)
                pe.matmul(bq_[g % 2][:], wkk[0:LAT, g], kvdt[0:LAT], start=True, stop=True).then_inc(k_done, 1)

            def select_scores(b, i):
                pe.wait_ge(qst_done, b * 4 + i + 1)
                pe.wait_ge(s0_done, b * 4 + i + 1)
                if not (isinstance(b, int) and isinstance(i, int)):
                    pe.wait_ge(qrope_done, b * 16 + 1 + 2)
                alone(pe)
                pe.matmul(bs[0][:], qst[0:SELD], ksel[0:SELD], start=True, stop=True).then_inc(ms_done, 1)

            def query(b, g, j):
                m = b * 16 + g * 4 + j
                pe.wait_ge(wq_in[j], (b * 4 + g) * 16 + 16)
                pe.wait_ge(qrope_done, m + 1)
                for c in range(DC):
                    mm = pe.matmul(query_bank(g, j)[:], wqs[:, j, c], xn3t[:, c], start=(c == 0), stop=(c == DC - 1))
                mm.then_inc(q_done, 1)

            def scores(b, g, j, o):
                t = TT - 1 - o
                m = b * 16 + g * 4 + j
                n = (t + 1) * P
                if o == 0:
                    pe.wait_ge(qr_done, m + 1 + 1)
                pe.wait_ge(ttr_done, m * 4 + o + 1)
                pe.matmul(bs[o % 2][:, 0:n], qr[:, j, t * P:(t + 1) * P],
                          kr[:, ds(g, 1), 0:n].rearrange("p o n -> p (o n)"), start=True, stop=True)\
                    .then_inc(s_done, 1)

            def head(b, g, j, more):
                m = b * 16 + g * 4 + j
                k = m * 4

                def transpose(o, t):
                    pe.wait_ge(exp_done, k + o + 1 + 2)
                    pe.wait_ge(pte_done, k + o + 1)
                    for i in range(t + 1):
                        mm = pe.transpose(bp[o % 2][:, i * P:(i + 1) * P], pr[:, t, i * P:(i + 1) * P], ident[:])
                    mm.then_inc(tp_done, 1)

                def values(o, t):
                    if o == 0:
                        pe.wait_ge(norm_done, m + 1)
                    pe.wait_ge(pte_done, k + o + 1 + 2)
                    for i in range(t + 1):
                        mm = pe.matmul(by[j % 2][:, t * AUG:(t + 1) * AUG], pt[:, o % 2, i * P:(i + 1) * P], kva[:, i],
                                       start=(o == 0 and i == 0), stop=(i == t), skip_group_check=True)
                    mm.then_inc(pv_done, 1)

                if not (isinstance(g, int) and g == 3 and j >= 2):
                    query(b, g + (j + 2) // 4, (j + 2) % 4)
                if final(g, j) and more:
                    selectors(b + 1)
                for o, t in tiles():
                    transpose(o, t)
                    if following(g, j):
                        scores(b, *following(g, j), o)
                    if o == 0 and at(g, j, 3, 2) and more:
                        pe.wait_ge(qrope_done, b * 16 + 16 + 2)
                        front(b + 1)
                    if o > 0:
                        values(*tiles()[o - 1])
                    if o == 1 and at(g, j, 3, 2) and more:
                        latents(b + 1)
                    if o % 2 == 1 and final(g, j) and more:
                        keys(b + 1, o // 2)
                values(*tiles()[TT - 1])

            def turn(b, t):
                for half in range(2):
                    pe.wait_ge(yte_done, b * 8 + t * 2 + half + 1)
                    for c in range(4):
                        hp = half * 4 + c
                        mm = pe.transpose(bp[half][:, c * P:(c + 1) * P],
                                          ym[:, t, hp * 2:hp * 2 + 2].rearrange("p h l -> p (h l)"), ident[:])
                    mm.then_inc(yt_done, 1)

            def project(b, t):
                pe.wait_ge(yte_done, b * 8 + t * 2 + 2 + 2)
                pe.wait_ge(x4_done, b * 4 + t + 1)
                for hp in range(NH // 2):
                    mm = pe.matmul(bs[t % 2][:, 0:D], yt[:, t % 2, hp], wvo[:, hp], start=(hp == 0),
                                   stop=(hp == NH // 2 - 1))
                mm.then_inc(o_done, 1)

            def output(b, more):
                pe.wait_ge(norm_done, b * 16 + 16 + 2)
                turn(b, 0)
                turn(b, 1)
                if more:
                    latent_rows(b + 1)
                for t in range(TT):
                    project(b, t)
                    if more and t < 2:
                        keys(b + 1, t + 2)
                    if t + 2 < TT:
                        turn(b, t + 2)
                for part, lo, hi in PARTS4:
                    if more:
                        pe.wait_ge(x4_done, b * 4 + part + 3 + 2)
                        alone(pe)
                        query(b + 1, 0, part)
                    turn4(b, part, lo, hi)
                pe.wait_ge(xn4lo_done, b * 2 + 2)
                for c in range(2):
                    for t in range(TT):
                        pe.matmul(bp[c][:, t * P:(t + 1) * P], zero_w[:], zero_w[:], start=(t == 0), stop=False,
                                  skip_group_check=True)

            def turn4(b, part, lo, hi):
                pe.wait_ge(xn4_done, b * 2 + part + 1)
                for c in range(2):
                    for t in range(lo, hi):
                        mm = pe.transpose(bp[c][:, t * P:(t + 1) * P], xn4[:, t, c::2], ident[:])
                    if part == 1:
                        mm.then_inc(t4_done, 1)

            def gate_up(b, g, j):
                f = b * 16 + g * 4 + j
                pe.wait_ge(wlo_done, f + 1)
                pe.wait_ge(gelu_done, f + 1)
                pe.wait_ge(inter_done, f + 1)
                for w, banks, done in ((0, bq_, g_done), (1, by, u_done)):
                    parts = [(part[:, j % 2, c, w], xn4_hi[:, c]) for c in range(2) for part in (w_hi, w_lo)]
                    parts += [(w_hi[:, j % 2, c, w], xn4_lo[:, c]) for c in range(2)]
                    for n, (lhs, rhs) in enumerate(parts):
                        mm = pe.matmul(banks[j % 2][:], lhs, rhs, start=(n == 0), stop=(n == 5))
                    mm.then_inc(done, 1)

            def down(b, g, j):
                f = b * 16 + g * 4 + j
                pe.wait_ge(inter_done, f + 1 + 2)
                at = 2 * FN + (g * 2 + j // 2) * D
                for t in range(TT):
                    mm = pe.matmul(bp[t // 2][:, (t % 2) * D:(t % 2 + 1) * D], it[:, j % 2, t * P:(t + 1) * P],
                                   wffn[:, j % 2, ds(at, D)], start=False, stop=False, skip_group_check=True)
                mm.then_inc(dn_done, 1)

            front(0)
            latents(0)
            selectors(0)
            select_scores(0, 0)
            latent_rows(0)
            for g in range(NKV):
                keys(0, g)
            pe.wait_ge(s0_done, 2)
            query(0, 0, 0)
            query(0, 0, 1)
            with pe.Fori(1, TT) as i:
                select_scores(0, i)

            def sequence(b, more):
                alone(pe)
                pe.wait_ge(kr_done, b * 4 + 4 + 1)
                pe.wait_ge(kva_done, b + 1)
                pe.wait_ge(s0_done, b * 4 + 4 + 1)
                for o in range(TT):
                    if o == 1:
                        pe.wait_ge(qrope_done, b * 16 + 2 + 2)
                    scores(b, 0, 0, o)
                pe.wait_ge(fo_done, b * 2 + 2)
                alone(pe)
                quads(pe, lambda g, j: head(b, g, j, more))
                output(b, more)
                if more:
                    pe.wait_ge(krope_done, b * 4 + 4 + 4 + 2)
                    pe.wait_ge(qksel_done, b * 2 + 4)
                    pe.wait_ge(kva_done, b + 2)
                gate_up(b, 0, 0)

                def chunk(g, j):
                    if j == 0 and more:
                        select_scores(b + 1, g)
                    if not (isinstance(g, int) and g == 3 and j == 3):
                        gate_up(b, g + (j + 1) // 4, (j + 1) % 4)
                    down(b, g, j)

                quads(pe, chunk)

            with pe.Fori(0, NB - 1) as b:
                sequence(b, True)
            sequence(NB - 1, False)

        @block.vector
        def _(ve):
            ve.sem_inc(x4_done, 2)
            ve.sem_inc(krope_done, 2)
            ve.sem_inc(qrope_done, 2)
            ve.sem_inc(ttr_done, 2)
            ve.sem_inc(norm_done, 2)
            ve.sem_inc(s0_done, 1)
            ve.sem_inc(inter_done, 2)
            ve.sem_inc(fo_done, 2)
            ve.sem_inc(out_done, 16)
            ve.wait_ge(c3, 3)

            def first_stats(b):
                ve.wait_ge(xs_done, b * 2 + 2)
                alone(ve)
                for t in range(TT):
                    ve.bn_stats(bnbuf[:, t], xs[:, t]).then_inc(stat3, 1)
                for t in range(TT):
                    ve.wait_ge(stat3, b * 4 + t + 1)
                    alone(ve)
                    ve.bn_aggr(mv3[:, t], bnbuf[:, t]).then_inc(agg3, 1)

            def first_norm(b):
                ve.wait_ge(agg3, b * 4 + 4)
                ve.tensor_scalar(veps3[:], mv3[:, :, 1], EPS, None, ALU.add).then_inc(ve3, 1)

            def first_scale(b):
                ve.wait_ge(rs3, b + 1)
                for t in range(TT):
                    ins = ve.tensor_scalar(xn3[:, t], xs[:, t], mv3[:, t, 0:1], rstd3[:, t:t + 1], ALU.subtract, ALU.mult)
                ins.then_inc(xn3_done, 1)

            def rotary(src, bias, ta, tb, done_a, done, n):
                ve.scalar_tensor_tensor(out=ta[:], in0=src[:], scalar=bias(0, P), in1=rcos[:], op0=ALU.add, op1=ALU.mult)\
                    .then_inc(done_a, 1)
                ve.scalar_tensor_tensor(out=tb[H2:P], in0=src[0:H2], scalar=bias(0, H2), in1=rsin[0:H2], op0=ALU.add,
                                        op1=ALU.mult).then_inc(done_a, 1)
                ve.scalar_tensor_tensor(out=tb[0:H2], in0=src[H2:P], scalar=bias(H2, P), in1=rsin[H2:P], op0=ALU.add,
                                        op1=ALU.mult).then_inc(done, 1)

            def keys(b, *groups):
                for g in groups:
                    n = b * 4 + g
                    ve.wait_ge(k_done, n + 1)
                    ve.wait_ge(kr_done, n + 1)
                    rotary(bq_[g % 2], lambda lo, hi: bk[lo:hi, g:g + 1], ka, kb, krope_a, krope_done, n)

            def query(b, g, j):
                n = b * 16 + g * 4 + j
                ve.wait_ge(q_done, n + 1)
                ve.wait_ge(qr_done, n + 1)
                if query_bank(g, j) is bs[0]:
                    ve.wait_ge(kr_done, b * 4 + 4 + 1)
                rotary(query_bank(g, j), lambda lo, hi: bq[lo:hi, ds(g * 4 + j, 1)], qa, qb, qrope_a, qrope_done, n)

            def masked(b, g, j, o):
                k = (b * 16 + g * 4 + j) * 4
                t = TT - 1 - o
                n = (t + 1) * P
                ve.wait_ge(s_done, k + o + 1)
                ve.wait_ge(exp_done, k + o + 1)
                alone(ve)
                ve.tensor_tensor_reduce(sm[:, o % 2, 0:n], bs[o % 2][:, 0:n], mask[:, t, 0:n], -QS, 3.0e38,
                                        ALU.add, ALU.min, nm[:, o % 2]).then_inc(ttr_done, 1)

            def head(b, g, j):
                m = b * 16 + g * 4 + j
                k = m * 4
                if not (isinstance(g, int) and g == 3 and j >= 2):
                    query(b, g + (j + 2) // 4, (j + 2) % 4)
                for o in range(TT):
                    if following(g, j):
                        masked(b, *following(g, j), o)
                ve.wait_ge(pv_done, k + 4 + 2)
                y = by[j % 2][:, 0:TT * AUG].rearrange("p (t l) -> p t l", l=AUG)
                ve.wait_ge(norm_done, m + 2)
                ve.reciprocal(rec[:], y[:, :, LAT]).then_inc(rec_done, 1)
                ve.wait_ge(rec_done, m + 1)
                ve.tensor_tensor(ym[:, :, ds(g * 4 + j, 1)].rearrange("p t o l -> p t (o l)"), y[:, :, 0:LAT],
                                 rec[:].unsqueeze(2).broadcast_to([P, TT, LAT]), ALU.mult).then_inc(norm_done, 1)

            def residual(b, t):
                if t == 0:
                    ve.wait_ge(xo_done, b + 1)
                ve.wait_ge(o_done, b * 4 + t + 1 + 2)
                ve.tensor_tensor(x4[:, t], bs[t % 2][:, 0:D], xo[:, t], ALU.add).then_inc(x4_done, 1)
                ve.wait_ge(x4_done, b * 4 + t + 1 + 2)
                ve.bn_stats(bnbuf4[:, t], x4[:, t]).then_inc(stat4, 1)
                ve.wait_ge(stat4, b * 4 + t + 1)
                alone(ve)
                ve.bn_aggr(mv4[:, t], bnbuf4[:, t]).then_inc(agg4, 1)

            def second_norm(b, part, lo, hi):
                ve.wait_ge(agg4, b * 4 + hi)
                ve.tensor_scalar(veps4[:, lo:hi], mv4[:, lo:hi, 1], EPS, None, ALU.add).then_inc(ve4, 1)

            def second_scale(b, part, lo, hi):
                ve.wait_ge(rs4, b * 2 + part + 1)
                ve.wait_ge(out_done, b * 16 + 16)
                for t in range(lo, hi):
                    ins = ve.tensor_scalar(xn4[:, t], x4[:, t], mv4[:, t, 0:1], rstd4[:, t:t + 1], ALU.subtract, ALU.mult)
                ins.then_inc(xn4_done, 1)

            def select_start(b, o):
                n = (TT - o) * P
                ve.wait_ge(ms_done, b * 4 + o + 1 + 1)
                ve.tensor_tensor(s0[:, 0:n], bs[0][:, 0:n], causal[:, o * P:o * P + n], ALU.add).then_inc(s0_done, 1)

            def select_round(b, o, r):
                n = (b * 4 + o) * (SELK // 8) + r
                w = (TT - o) * P
                src = s0[:, 0:w] if r == 0 else sr[:, (r - 1) % 2, 0:w]
                if r == 0:
                    ve.wait_ge(s0_done, b * 4 + o + 1 + 1)
                else:
                    ve.wait_ge(mr_done, n)
                alone(ve)
                ve.max(m8[:], src).then_inc(mx_done, 1)
                ve.wait_ge(mx_done, n + 1)
                alone(ve)
                ve.match_replace(sr[:, r % 2, 0:w], m8[:], src, GONE).then_inc(mr_done, 1)

            def select_end(b, o):
                n = b * 4 + o + 1
                w = (TT - o) * P
                ve.wait_ge(mr_done, n * (SELK // 8))
                ve.tensor_tensor(eq[:, 0:w], sr[:, (SELK // 8 - 1) % 2, 0:w], s0[:, 0:w], ALU.is_equal).then_inc(eq_done, 1)
                ve.wait_ge(eq_done, n)
                ve.tensor_tensor(eo[:, 0:w], eq[:, 0:w], offdiag[:, o * P:o * P + w], ALU.mult).then_inc(eo_done, 1)
                ve.wait_ge(eo_done, n)
                ve.tensor_tensor(mask[:, TT - 1 - o, 0:w], eo[:, 0:w], causal[:, o * P:o * P + w], ALU.add)\
                    .then_inc(mask_done, 1)

            def hidden(b, g, j):
                f = b * 16 + g * 4 + j
                ve.wait_ge(u_done, f + 1)
                ve.wait_ge(gelu_done, f + 1 + 2)
                ve.wait_ge(dn_done, f + 1)
                ve.tensor_tensor(it[:, j % 2], by[j % 2][:], gl[:, j % 2], ALU.mult).then_inc(inter_done, 1)

            first_stats(0)
            first_norm(0)
            first_scale(0)
            for o in range(TT):
                select_start(0, o)
                for r in range(SELK // 8):
                    select_round(0, o, r)
                    if o == 0 and r % 2 == 1:
                        keys(0, r // 2)
                if o == 0:
                    query(0, 0, 0)
                select_end(0, o)
            query(0, 0, 1)
            ve.wait_ge(mask_done, 4)
            for o in range(TT):
                masked(0, 0, 0, o)

            def sequence(b, more):
                def step(g, j):
                    if more and final(g, j):
                        keys(b + 1, 0)
                    head(b, g, j)
                    if more and at(g, j, 3, 0):
                        first_stats(b + 1)
                        first_norm(b + 1)
                    if more and at(g, j, 3, 1):
                        first_scale(b + 1)
                    if more and final(g, j):
                        keys(b + 1, 1)

                quads(ve, step)
                for t in range(TT):
                    residual(b, t)
                    for part, lo, hi in PARTS4:
                        if hi == t + 1:
                            second_norm(b, part, lo, hi)
                    if more and t < 2:
                        keys(b + 1, t + 2)
                    if t >= TT - 2:
                        second_scale(b, *PARTS4[t - TT + 2])
                for c in range(2):
                    ve.wait_ge(xn4hi_done, b * 2 + c + 1)
                    ve.tensor_tensor(xn4_lo[:, c], bp[c][:], xn4_hi[:, c].bitcast(F32), ALU.subtract)\
                        .then_inc(xn4lo_done, 1)
                if more:
                    query(b + 1, 0, 0)
                    query(b + 1, 0, 1)

                rounds = ((0, 1), (2, 3), (4, 5), (6, 7))
                for g in range(4):
                    for j in range(4):
                        if j == 0 and more:
                            select_start(b + 1, g)
                        hidden(b, g, j)
                        if more:
                            for r in rounds[j]:
                                select_round(b + 1, g, r)
                            if j == 3:
                                select_end(b + 1, g)
                if more:
                    ve.wait_ge(mask_done, b * 4 + 4 + 4)
                    masked(b + 1, 0, 0, 0)
                    masked(b + 1, 0, 0, 1)
                ve.wait_ge(dn_done, b * 16 + 16 + 2)
                ve.wait_ge(out_done, b * 16 + 16)
                for half in range(2):
                    t0 = half * 2
                    ve.tensor_tensor(ob[:, t0:t0 + 2].rearrange("p t d -> p (t d)"), bp[half][:],
                                     x4[:, t0:t0 + 2].rearrange("p t d -> p (t d)"), ALU.add).then_inc(fo_done, 1)
                if more:
                    masked(b + 1, 0, 0, 2)
                    masked(b + 1, 0, 0, 3)

            with ve.Fori(0, NB - 1) as b:
                sequence(b, True)
            sequence(NB - 1, False)

        block.__exit__(None, None, None)
        sp.clear()


def lay_out(inputs):
    t = dict(inputs)
    a = {n: t[n] for n in ("L0_attn_x", "L0_attn_D_skip")}
    a["b_dt"] = t["L0_attn_b_dt"].reshape(DC, P).T
    a["a_log"] = t["L0_attn_A_log"].reshape(DC, P).T
    a["w_dt_t"] = t["L0_attn_W_dt"].T
    a["w_b_t"] = t["L0_attn_W_B"].T
    a["w_c_t"] = t["L0_attn_W_C"].T
    a["w_r_t"] = t["L0_ffn_router_weight"].T
    order = np.arange(FN).reshape(FN // 2 // P, P, 2).transpose(0, 2, 1).reshape(-1)
    jc = FN // 2 // P
    down = t["L1_ffn_down_W_packed"].T.reshape(jc, P, D).transpose(1, 0, 2).reshape(P, FN)
    a["codes"] = np.concatenate([t["L1_ffn_gate_W_packed"][order].T, t["L1_ffn_up_W_packed"][order].T, down], 1)
    down_s = t["L1_ffn_down_scales"].T.reshape(jc, P // 16, D).transpose(1, 0, 2).reshape(P // 16, FN)
    a["scales"] = np.concatenate([t["L1_ffn_gate_scales"][order].T, t["L1_ffn_up_scales"][order].T, down_s], 1)
    pair = np.concatenate([np.arange(0, HD, 2), np.arange(1, HD, 2)])
    wku, bku = t["L1_attn_Wku"], t["L1_attn_bku"]
    kd = NKV * HD
    a["wq"] = t["L1_attn_Wq"].reshape(D, NH, HD)[:, :, pair].reshape(D, NH * HD)
    a["wqsel"] = t["L1_attn_Wq"][:, :SELD]
    a["wkk"] = wku[:, :kd].reshape(LAT, NKV, HD)[:, :, pair].reshape(LAT, kd)
    a["wksel"] = wku[:, :SELD]
    a["wvt"] = wku[:, kd:].reshape(LAT, NKV, HD).transpose(2, 1, 0)
    a["bq"] = t["L1_attn_bq"].reshape(NH, HD)[:, pair].T
    a["bk"] = bku[:kd].reshape(NKV, HD)[:, pair].T
    a["bv"] = bku[kd:].reshape(NKV, HD).T
    a["bkd"] = t["L1_attn_bkd"][:, None]
    a["bqsel"] = t["L1_attn_bq"][:SELD, None]
    a["bksel"] = bku[:SELD, None]
    for n in ("L1_attn_Wkd", "L1_attn_Wo", "L1_attn_bo"):
        a[n] = t[n]
    inv = np.float32(1.0) / np.float32(10000.0) ** (np.arange(0, HD, 2, dtype=np.float32) / np.float32(HD))
    angle = np.arange(S, dtype=np.float32)[:, None] * inv[None, :]
    angle = np.concatenate([angle, angle], 1)[:, ::2].T.astype(np.float32)
    a["rcos"] = np.concatenate([np.cos(angle), np.cos(angle)], 0)
    a["rsin"] = np.concatenate([np.sin(angle), -np.sin(angle)], 0)
    a["L0_ffn_gate_up_proj"] = t["L0_ffn_gate_up_proj"]
    a["L0_ffn_down_proj"] = t["L0_ffn_down_proj"]
    return {n: np.ascontiguousarray(v) for n, v in a.items()}


def program(nc, a, out):
    acc = [nc.dram_tensor(f"acc{c}", (T, D), F32, kind="Internal").ap() for c in range(NCH)]
    xg = nc.dram_tensor("rows_for_experts", (T, ROW), F32, kind="Internal").ap()
    with ExitStack() as st:
        sb = Space(nc, st).sb
        slots = sb("slots", [P, NE, 2], I32)
        work = sb("work", [P, 2 * 3 * FN])
        codes, scales = work[:, 0:3 * FN].bitcast(I32), work[:, 3 * FN:]
        stage1(nc, a, acc, xg, slots, codes, scales)
        wffn = sb("wffn", [P, 2, 3 * FN])
        shapes = dict(wq=(DC, NH * HD), wqsel=(DC, SELD), wkd=(DC, LAT), wkk=(NKV, HD), wksel=(SELD,), bq=(NH,),
                      bk=(NKV,), bkd=(1,), bqsel=(1,), bksel=(1,), rcos=(S,), rsin=(S,), wvo=(NH // 2, D), obias=(D,))
        w = {n: sb(n, [P, *shape]) for n, shape in shapes.items()}
        stage2(nc, a, acc, xg, slots, codes, scales, wffn, w)
        stage3(nc, acc, wffn, w, work, out)


def kernel(**inputs):
    import concourse.bacc as bacc
    from concourse.bass_utils import run_bass_kernel_spmd

    arrays = lay_out({n: np.asarray(v) for n, v in inputs.items()})
    nc = bacc.Bacc("TRN2", target_bir_lowering=False, num_devices=1)
    a = {n: nc.dram_tensor(f"in_{n}", v.shape, mybir.dt.from_np(v.dtype), kind="ExternalInput").ap()
         for n, v in arrays.items()}
    out = nc.dram_tensor("out", (NB, S, D), F32, kind="ExternalOutput").ap()
    program(nc, a, out)
    r = run_bass_kernel_spmd(nc, [{f"in_{n}": v for n, v in arrays.items()}], core_ids=[0])
    return r.results[0]["out"]
```
